# Optimizing a Trainium2 kernel written in Bass

```python
import numpy as np
import jax
import jax.numpy as jnp

def _softmax(x, axis=-1):
    return jax.nn.softmax(x, axis=axis)

def _gelu(x):
    return jax.nn.gelu(x, approximate=True)

def _silu(x):
    return jax.nn.silu(x)

def _sigmoid(x):
    return jax.nn.sigmoid(x)

def _layernorm(x, axis=-1, eps=1e-05):
    m = jnp.mean(x, axis=axis, keepdims=True)
    v = jnp.var(x, axis=axis, keepdims=True)
    return (x - m) / jnp.sqrt(v + eps)

def _scatter_add(tgt, idx, src, axis=0):
    return tgt.at[idx].add(src)

def _segment_sum(src, seg, n):
    return jax.ops.segment_sum(src, seg, n)
kernel_name = 'mk_adj_preln_d4_adj_r2_1e66c8'

def setup_inputs(seed: int=0):
    np.random.seed(seed)
    _w = jnp.asarray

    def _rec_inputs():
        import jax
        import jax.numpy as jnp
        _gk = jax.random.key(seed)
        x = -7.109e-05 + 0.9999 * jax.random.normal(jax.random.fold_in(_gk, 1), (128, 64, 256), jnp.float32)
        _a = jax.random.bernoulli(jax.random.fold_in(_gk, 2), 0.0625, (128, 64, 64))
        adj = _a
        return (x, adj)
    x, adj = _rec_inputs()

    def _L0_gnn_setup():
        import jax, jax.numpy as jnp
        import numpy as np
        B, S, D, H = (1024, 64, 256, 8)
        HD = D // H
        SCALE = float(1.0 / np.sqrt(HD))

        def _static_masks():
            sq = np.arange(64)
            r = sq // 8
            f = sq % 8
            ri, rj = (r[:, None], r[None, :])
            fi, fj = (f[:, None], f[None, :])
            dr = np.abs(ri - rj)
            df = np.abs(fi - fj)
            eye = np.eye(64, dtype=bool)
            file_m = fi == fj
            rank_m = ri == rj
            diag_m = ri - fi == rj - fj
            adiag_m = ri + fi == rj + fj
            knight_m = (dr == 2) & (df == 1) | (dr == 1) & (df == 2) | eye
            king_m = (dr <= 1) & (df <= 1)
            return np.stack([file_m, rank_m, diag_m, adiag_m, knight_m, king_m])
        STATIC = jnp.asarray(_static_masks())
        EYE = jnp.eye(S, dtype=bool)
        key = jax.random.key(seed)
        ks = jax.random.split(key, 7)
        x = jax.random.normal(ks[0], (B, S, D), jnp.float32)
        ray_mask = jax.random.bernoulli(ks[1], 0.15, (B, S, S))
        attack_mask = jax.random.bernoulli(ks[2], 0.1, (B, S, S))
        s = 1.0 / np.sqrt(D)

        def lin(k):
            k1, k2 = jax.random.split(k)
            W = jax.random.uniform(k1, (D, D), jnp.float32, -s, s)
            b = jax.random.uniform(k2, (D,), jnp.float32, -s, s)
            return (W, b)
        Wq, bq = lin(ks[3])
        Wk, bk = lin(ks[4])
        Wv, bv = lin(ks[5])
        Wo, bo = lin(ks[6])
        return dict(x=x, ray_mask=ray_mask, attack_mask=attack_mask, Wq=Wq, bq=bq, Wk=Wk, bk=bk, Wv=Wv, bv=bv, Wo=Wo, bo=bo)
    _L0_gnn_all = _L0_gnn_setup()
    _L0_gnn_in = {k: v for k, v in _L0_gnn_all.items() if k in ('Wq', 'bq', 'Wk', 'bk', 'Wv', 'bv', 'Wo', 'bo')}
    del _L0_gnn_all

    def _L1_gnn_setup():
        import jax, jax.numpy as jnp
        import numpy as np
        QUERY_DIM = 256
        HEADS = 4
        DIM_HEAD = 64
        INNER = HEADS * DIM_HEAD
        B, N = (4, 1024)
        key = jax.random.key(seed)
        ks = jax.random.split(key, 6)
        s = 1.0 / np.sqrt(QUERY_DIM)
        x = jax.random.normal(ks[0], (B, N, QUERY_DIM), dtype=jnp.float32)
        adjacency_mask = jax.random.randint(ks[1], (B, N, N), 0, 2) > 0
        Wq = jax.random.normal(ks[2], (QUERY_DIM, INNER), dtype=jnp.float32) * s
        Wk = jax.random.normal(ks[3], (QUERY_DIM, INNER), dtype=jnp.float32) * s
        Wv = jax.random.normal(ks[4], (QUERY_DIM, INNER), dtype=jnp.float32) * s
        Wo = jax.random.normal(ks[5], (INNER, QUERY_DIM), dtype=jnp.float32) * (1.0 / np.sqrt(INNER))
        bo = jnp.zeros((QUERY_DIM,), dtype=jnp.float32)
        return {'x': x, 'adjacency_mask': adjacency_mask, 'Wq': Wq, 'Wk': Wk, 'Wv': Wv, 'Wo': Wo, 'bo': bo}
    _L1_gnn_all = _L1_gnn_setup()
    _L1_gnn_in = {k: v for k, v in _L1_gnn_all.items() if k in ('Wq', 'Wk', 'Wv', 'Wo', 'bo')}
    del _L1_gnn_all

    def _L2_gnn_setup():
        import jax, jax.numpy as jnp
        import numpy as np
        B, N, IN, OUT, H = (16, 512, 256, 256, 4)
        key = jax.random.key(seed)
        ks = jax.random.split(key, 10)
        s = 0.03
        return {'h': jax.random.normal(ks[0], (B, N, IN), jnp.float32), 'adj': jax.random.randint(ks[1], (B, N, N), 0, 2) > 0, 'W': jax.random.normal(ks[2], (H, OUT, IN), jnp.float32) * s, 'bW': jax.random.normal(ks[3], (H, OUT), jnp.float32) * s, 'attn': jax.random.normal(ks[4], (H, OUT, OUT), jnp.float32) * s, 'A_w': jax.random.normal(ks[5], (OUT, OUT * H), jnp.float32) * s, 'fc_w': jax.random.normal(ks[6], (OUT, IN), jnp.float32) * s, 'g1_w': jax.random.normal(ks[7], (OUT, OUT), jnp.float32) * s, 'g2_w': jax.random.normal(ks[8], (OUT, OUT), jnp.float32) * s, 'gbias': jax.random.normal(ks[9], (OUT,), jnp.float32) * s}
    _L2_gnn_all = _L2_gnn_setup()
    _L2_gnn_in = {k: v for k, v in _L2_gnn_all.items() if k in ('W', 'bW', 'attn', 'A_w', 'fc_w', 'g1_w', 'g2_w', 'gbias')}
    del _L2_gnn_all

    def _L3_gnn_setup():
        import jax, jax.numpy as jnp
        import numpy as np
        HEAD_NUM = 8
        THRESHOLD = 0.1
        NEG = -10000000000.0
        COS_EPS = 1e-08
        B, S, D = (8, 512, 256)
        D_OUT = 256
        key = jax.random.key(seed)
        ks = jax.random.split(key, 12)
        embs = jax.random.normal(ks[0], (B, S, D), dtype=jnp.float32)
        lengths = jax.random.randint(ks[1], (B,), S // 2, S + 1)
        pad = jnp.arange(S)[None, :] >= lengths[:, None]
        score_mask = pad[:, :, None] | pad[:, None, :]
        sc = 1.0 / np.sqrt(D)
        mk = lambda k, shp: jax.random.normal(k, shp, dtype=jnp.float32) * sc
        return {'embs': embs, 'score_mask': score_mask, 'map_w': mk(ks[2], (D, D)), 'map_b': jnp.zeros((D,), jnp.float32), 'q_w': mk(ks[3], (D, D)), 'q_b': jnp.zeros((D,), jnp.float32), 'k_w': mk(ks[4], (D, D)), 'k_b': jnp.zeros((D,), jnp.float32), 'gcn_map_w': mk(ks[5], (D_OUT, D)), 'gcn_map_b': jnp.zeros((D_OUT,), jnp.float32), 'gcn_W': jax.random.normal(ks[6], (D_OUT // HEAD_NUM, D_OUT // HEAD_NUM), dtype=jnp.float32) * (1.0 / np.sqrt(D_OUT // HEAD_NUM))}
    _L3_gnn_all = _L3_gnn_setup()
    _L3_gnn_in = {k: v for k, v in _L3_gnn_all.items() if k in ('map_w', 'map_b', 'q_w', 'q_b', 'k_w', 'k_b', 'gcn_map_w', 'gcn_map_b', 'gcn_W')}
    del _L3_gnn_all
    return {'x': x, 'adj': adj, 'L0_gnn_Wq': _L0_gnn_in['Wq'], 'L0_gnn_bq': _L0_gnn_in['bq'], 'L0_gnn_Wk': _L0_gnn_in['Wk'], 'L0_gnn_bk': _L0_gnn_in['bk'], 'L0_gnn_Wv': _L0_gnn_in['Wv'], 'L0_gnn_bv': _L0_gnn_in['bv'], 'L0_gnn_Wo': _L0_gnn_in['Wo'], 'L0_gnn_bo': _L0_gnn_in['bo'], 'L1_gnn_Wq': _L1_gnn_in['Wq'], 'L1_gnn_Wk': _L1_gnn_in['Wk'], 'L1_gnn_Wv': _L1_gnn_in['Wv'], 'L1_gnn_Wo': _L1_gnn_in['Wo'], 'L1_gnn_bo': _L1_gnn_in['bo'], 'L2_gnn_W': _L2_gnn_in['W'], 'L2_gnn_bW': _L2_gnn_in['bW'], 'L2_gnn_attn': _L2_gnn_in['attn'], 'L2_gnn_A_w': _L2_gnn_in['A_w'], 'L2_gnn_fc_w': _L2_gnn_in['fc_w'], 'L2_gnn_g1_w': _L2_gnn_in['g1_w'], 'L2_gnn_g2_w': _L2_gnn_in['g2_w'], 'L2_gnn_gbias': _L2_gnn_in['gbias'], 'L3_gnn_map_w': _L3_gnn_in['map_w'], 'L3_gnn_map_b': _L3_gnn_in['map_b'], 'L3_gnn_q_w': _L3_gnn_in['q_w'], 'L3_gnn_q_b': _L3_gnn_in['q_b'], 'L3_gnn_k_w': _L3_gnn_in['k_w'], 'L3_gnn_k_b': _L3_gnn_in['k_b'], 'L3_gnn_gcn_map_w': _L3_gnn_in['gcn_map_w'], 'L3_gnn_gcn_map_b': _L3_gnn_in['gcn_map_b'], 'L3_gnn_gcn_W': _L3_gnn_in['gcn_W']}

def reference(x, adj, L0_gnn_Wq, L0_gnn_bq, L0_gnn_Wk, L0_gnn_bk, L0_gnn_Wv, L0_gnn_bv, L0_gnn_Wo, L0_gnn_bo, L1_gnn_Wq, L1_gnn_Wk, L1_gnn_Wv, L1_gnn_Wo, L1_gnn_bo, L2_gnn_W, L2_gnn_bW, L2_gnn_attn, L2_gnn_A_w, L2_gnn_fc_w, L2_gnn_g1_w, L2_gnn_g2_w, L2_gnn_gbias, L3_gnn_map_w, L3_gnn_map_b, L3_gnn_q_w, L3_gnn_q_b, L3_gnn_k_w, L3_gnn_k_b, L3_gnn_gcn_map_w, L3_gnn_gcn_map_b, L3_gnn_gcn_W):
    import jax
    import jax.numpy as jnp

    def _L0_gnn_ref(x, ray_mask, attack_mask, Wq, bq, Wk, bk, Wv, bv, Wo, bo):
        import jax, jax.numpy as jnp
        import numpy as np
        B, S, D, H = (1024, 64, 256, 8)
        HD = D // H
        SCALE = float(1.0 / np.sqrt(HD))

        def _static_masks():
            sq = np.arange(64)
            r = sq // 8
            f = sq % 8
            ri, rj = (r[:, None], r[None, :])
            fi, fj = (f[:, None], f[None, :])
            dr = np.abs(ri - rj)
            df = np.abs(fi - fj)
            eye = np.eye(64, dtype=bool)
            file_m = fi == fj
            rank_m = ri == rj
            diag_m = ri - fi == rj - fj
            adiag_m = ri + fi == rj + fj
            knight_m = (dr == 2) & (df == 1) | (dr == 1) & (df == 2) | eye
            king_m = (dr <= 1) & (df <= 1)
            return np.stack([file_m, rank_m, diag_m, adiag_m, knight_m, king_m])
        STATIC = jnp.asarray(_static_masks())
        EYE = jnp.eye(S, dtype=bool)
        Bn = x.shape[0]

        def split_heads(t):
            return t.reshape(Bn, S, H, HD).transpose(0, 2, 1, 3)
        q = split_heads(x @ Wq.T + bq)
        k = split_heads(x @ Wk.T + bk)
        v = split_heads(x @ Wv.T + bv)
        scores = jnp.einsum('bhsd,bhtd->bhst', q, k) * SCALE
        mask = jnp.concatenate([jnp.broadcast_to(STATIC[None], (Bn, 6, S, S)), (ray_mask | EYE)[:, None], (attack_mask | EYE)[:, None]], axis=1)
        scores = jnp.where(mask, scores, jnp.float32(-1000000000.0))
        attn = jax.nn.softmax(scores, axis=-1)
        out = jnp.einsum('bhst,bhtd->bhsd', attn, v)
        out = out.transpose(0, 2, 1, 3).reshape(Bn, S, D)
        return out @ Wo.T + bo

    def _L1_gnn_ref(x, adjacency_mask, Wq, Wk, Wv, Wo, bo):
        import jax, jax.numpy as jnp
        import numpy as np
        QUERY_DIM = 256
        HEADS = 4
        DIM_HEAD = 64
        INNER = HEADS * DIM_HEAD
        B, N = (4, 1024)
        scale = DIM_HEAD ** (-0.5)

        def split_heads(t):
            b, n, _ = t.shape
            return t.reshape(b, n, HEADS, DIM_HEAD).transpose(0, 2, 1, 3)
        q = split_heads(x @ Wq)
        k = split_heads(x @ Wk)
        v = split_heads(x @ Wv)
        sim = jnp.einsum('bhid,bhjd->bhij', q, k) * scale
        neg = -jnp.finfo(sim.dtype).max
        sim = jnp.where(adjacency_mask[:, None, :, :], sim, neg)
        attn = jax.nn.softmax(sim, axis=-1)
        out = jnp.einsum('bhij,bhjd->bhid', attn, v)
        out = out.transpose(0, 2, 1, 3).reshape(x.shape[0], x.shape[1], INNER)
        return out @ Wo + bo

    def _L2_gnn_ref(h, adj, W, bW, attn, A_w, fc_w, g1_w, g2_w, gbias):
        import jax, jax.numpy as jnp
        import numpy as np
        B, N, IN, OUT, H = (16, 512, 256, 256, 4)
        Wh = jnp.einsum('bni,hoi->bhno', h, W) + bW[None, :, None, :]
        e = jnp.einsum('bhno,hop->bhnp', Wh, attn)
        scores = jnp.einsum('bhnp,bhmp->bhnm', e, Wh)
        A_mat = jnp.tanh(jnp.where(adj[:, None, :, :], scores, 0.0))
        hp = jax.nn.relu(jnp.einsum('bhnm,bhmo->bhno', A_mat, Wh))
        cat = jnp.transpose(hp, (0, 2, 1, 3)).reshape(hp.shape[0], hp.shape[2], -1)
        ha = cat @ A_w.T
        hf = h @ fc_w.T
        coeff = jax.nn.sigmoid(hf @ g1_w.T + ha @ g2_w.T + gbias)
        return hf * coeff + ha * (1.0 - coeff)

    def _L3_gnn_ref(embs, score_mask, map_w, map_b, q_w, q_b, k_w, k_b, gcn_map_w, gcn_map_b, gcn_W):
        import jax, jax.numpy as jnp
        import numpy as np
        HEAD_NUM = 8
        THRESHOLD = 0.1
        NEG = -10000000000.0
        COS_EPS = 1e-08
        B, S, D = (8, 512, 256)
        D_OUT = 256
        b, s, d = embs.shape
        h, dk = (HEAD_NUM, d // HEAD_NUM)
        sm = score_mask[:, None, :, :]
        keep = (~sm[..., 0:1]).astype(embs.dtype)
        m = embs @ map_w.T + map_b
        sem = m.reshape(b, s, h, dk).transpose(0, 2, 1, 3)
        norm = jnp.maximum(jnp.linalg.norm(sem, axis=-1, keepdims=True), COS_EPS)
        n = sem / norm
        cos = jnp.einsum('bhsd,bhtd->bhst', n, n)
        cos = cos * (~sm).astype(cos.dtype)
        cos_adj = (cos > THRESHOLD).astype(embs.dtype)
        q = (m @ q_w.T + q_b).reshape(b, s, h, dk).transpose(0, 2, 1, 3)
        k = (m @ k_w.T + k_b).reshape(b, s, h, dk).transpose(0, 2, 1, 3)
        scores = jnp.einsum('bhsd,bhtd->bhst', q, k) / jnp.sqrt(jnp.asarray(dk, embs.dtype))
        scores = jnp.where(sm, NEG, scores)
        p_attn = jax.nn.softmax(scores, axis=-1) * keep
        adj = cos_adj * p_attn
        hk = gcn_map_w.shape[0] // h
        sem_h = (embs @ gcn_map_w.T + gcn_map_b).reshape(b, s, h, hk).transpose(2, 0, 1, 3)
        adj_h = adj.transpose(1, 0, 2, 3)
        Ax = jnp.einsum('hbst,hbtd->hbsd', adj_h, sem_h)
        AxW = Ax @ gcn_W.T
        denom = adj_h.sum(-1, keepdims=True) + 1.0
        out = jax.nn.relu(AxW / denom)
        out = out.transpose(1, 2, 0, 3).reshape(b, s, h * hk)
        return out
    h = jnp.maximum(_layernorm(x, axis=-1), 0.0)
    x = x + _L0_gnn_ref(h, adj, adj, L0_gnn_Wq, L0_gnn_bq, L0_gnn_Wk, L0_gnn_bk, L0_gnn_Wv, L0_gnn_bv, L0_gnn_Wo, L0_gnn_bo)
    h = jnp.maximum(_layernorm(x, axis=-1), 0.0)
    x = x + _L1_gnn_ref(h, adj, L1_gnn_Wq, L1_gnn_Wk, L1_gnn_Wv, L1_gnn_Wo, L1_gnn_bo)
    h = jnp.maximum(_layernorm(x, axis=-1), 0.0)
    x = x + _L2_gnn_ref(h, adj, L2_gnn_W, L2_gnn_bW, L2_gnn_attn, L2_gnn_A_w, L2_gnn_fc_w, L2_gnn_g1_w, L2_gnn_g2_w, L2_gnn_gbias)
    h = jnp.maximum(_layernorm(x, axis=-1), 0.0)
    x = x + _L3_gnn_ref(h, adj, L3_gnn_map_w, L3_gnn_map_b, L3_gnn_q_w, L3_gnn_q_b, L3_gnn_k_w, L3_gnn_k_b, L3_gnn_gcn_map_w, L3_gnn_gcn_map_b, L3_gnn_gcn_W)
    return x

_drawn_inputs = setup_inputs


def setup_inputs(seed=0):
    import zlib

    import numpy as np

    out = dict(_drawn_inputs(seed))
    spreads = {'L1_gnn_bo': (0.0, 0.1),
     'L3_gnn_map_b': (0.0, 0.8),
     'L3_gnn_q_b': (0.0, 0.8),
     'L3_gnn_k_b': (0.0, 0.8),
     'L3_gnn_gcn_map_b': (0.0, 0.292)}
    factors = {'L0_gnn_Wq': 5.791,
     'L0_gnn_bq': 8.0,
     'L0_gnn_Wk': 5.698,
     'L0_gnn_bk': 8.0,
     'L0_gnn_bv': 2.733,
     'L2_gnn_g1_w': 3.398,
     'L2_gnn_g2_w': 3.06,
     'L2_gnn_gbias': 8.0,
     'L3_gnn_map_w': 5.15,
     'L3_gnn_q_w': 6.148,
     'L3_gnn_k_w': 6.115}
    for name, (base, spread) in spreads.items():
        noise = np.random.default_rng([zlib.crc32(name.encode()), seed]).standard_normal(out[name].shape)
        drawn = base * np.exp(spread * noise) if base else spread * noise
        out[name] = jnp.asarray(drawn.astype(out[name].dtype))
    for name, factor in factors.items():
        out[name] = (out[name] * factor).astype(out[name].dtype)
    return out
```

```python
from contextlib import ExitStack

import numpy as np

import concourse.bass as bass
from concourse import mybir

ALU = mybir.AluOpType
ACT = mybir.ActivationFunctionType
AX = mybir.AxisListType
F32 = mybir.dt.float32
F32R = mybir.dt.float32r
BF16 = mybir.dt.bfloat16
U8 = mybir.dt.uint8

P = 128
S = 64
D = 256
KC = D // P
PAIRS = 2
TOK = PAIRS * P
NB = TOK // S
BANK = 512
MASKED = float(2.0 ** 100)
LN_EPS = 1e-5
GROUPS = 32


class Signal:

    def __init__(self, sem, per_group):
        self.sem, self.per_group, self.base = sem, per_group, 0

    def layer_done(self, groups):
        self.base += groups * self.per_group


class Group:

    def __init__(self, reg, c):
        self.reg, self.c, self.slot = reg, c, c % 2

    def back(self, k):
        return Group(self.reg, self.c - k)

    def times(self, n):
        return self.c * n if self.reg is None else self.reg * (2 * n) + self.c * n

    def exists(self, groups):
        return self.reg is not None or 0 <= self.c < groups


def after(eng, signal, g, k=None, apart=None):
    k = signal.per_group if k is None else k
    c = g.c
    if g.reg is None and c >= GROUPS:
        c, k = GROUPS - 1, signal.per_group
    const = signal.base + signal.per_group * c + k
    if g.reg is not None:
        eng.wait_ge(signal.sem, g.reg * (2 * signal.per_group) + const)
        if apart is not None:
            eng.sem_inc(apart.waits_passed.sem, 1)
    elif c >= 0:
        eng.wait_ge(signal.sem, const)


def after_dma(eng, signals, g, apart=None):
    signal = signals[g.slot]
    const = signal.base + 8 * (g.c - g.slot) + 16
    if g.reg is None:
        if g.c >= 0:
            eng.wait_ge(signal.sem, const)
    else:
        eng.wait_ge(signal.sem, g.reg * 16 + const)
        if apart is not None:
            eng.sem_inc(apart.waits_passed.sem, 1)


def run_steps(eng, step, groups, lag):
    head = (lag + 3) // 2 * 2
    body = (groups - head) // 2 * 2
    for s in range(head):
        step(Group(None, s))
    with eng.Fori(head // 2, (head + body) // 2) as i:
        step(Group(i, 0))
        step(Group(i, 1))
    for s in range(head + body, groups + lag):
        step(Group(None, s))


class Core:

    def __init__(self, nc, ctx, groups):
        self.nc, self.ctx, self.groups = nc, ctx, groups
        self.signals = {}
        self.dma_signals = {}
        self.counters = {}
        self.ps = ctx.enter_context(nc.psum_tensor("banks", [P, 8, BANK], F32))

    def named_signal(self, name, per_group=1):
        if name not in self.signals:
            self.signals[name] = Signal(self.ctx.enter_context(self.nc.semaphore(name)), per_group)
        assert self.signals[name].per_group == per_group, name
        return self.signals[name]

    def named_dma_signal(self, name):
        if name not in self.dma_signals:
            self.dma_signals[name] = [Signal(self.ctx.enter_context(self.nc.semaphore(f"{name}_{i}")), 8)
                                      for i in range(2)]
        return self.dma_signals[name]

    def once(self, name):
        if name not in self.counters:
            self.counters[name] = Once(self.ctx.enter_context(self.nc.semaphore(name)))
        return self.counters[name]

    def wait_constants(self, eng):
        eng.wait_ge(self.constants_ready.sem, 1)

    def end_layer(self, used):
        for n in used:
            if n in self.signals:
                self.signals[n].layer_done(self.groups)
            else:
                for s in self.dma_signals[n]:
                    s.layer_done(self.groups)


class Once:

    def __init__(self, sem):
        self.sem = sem


def tokens_of(dram, g):
    return dram[bass.ds(g.times(TOK), TOK), :].rearrange("(p q) d -> q p d", q=P)


def mm3(nc, out, lo_hi_t, lo_hi, start, stop, lhs, rhs):
    (lh, ll), (rh, rl) = lo_hi_t, lo_hi
    nc.tensor.matmul(out, lhs(lh), rhs(rh), start=start, stop=False, skip_group_check=True)
    nc.tensor.matmul(out, lhs(lh), rhs(rl), start=False, stop=False, skip_group_check=True)
    return nc.tensor.matmul(out, lhs(ll), rhs(rh), start=False, stop=stop, skip_group_check=True)


class LayerNorm:

    def __init__(self, core, ctx, tag, x_dram, want_f32=False):
        nc = core.nc
        sb = lambda n, shape, dt=F32: ctx.enter_context(nc.sbuf_tensor(f"{tag}_{n}", shape, dt))
        self.core, self.nc, self.x_dram, self.want_f32 = core, nc, x_dram, want_f32
        self.x = sb("x", [P, 2, PAIRS, D])
        self.stats = sb("stats", [P, 2, PAIRS, 6])
        self.mean_var = sb("mean_var", [P, 2, PAIRS, 2])
        self.var_eps = sb("var_eps", [P, 2, PAIRS])
        self.rstd = sb("rstd", [P, 2, PAIRS])
        self.shift = sb("shift", [P, 2, PAIRS])
        self.h = sb("h", [P, 2, PAIRS, D])
        self.hT_hi = sb("hT_hi", [P, 2, KC, TOK], F32R)
        self.hT_lo = sb("hT_lo", [P, 2, KC, TOK], F32R)
        self.hT = sb("hT", [P, 2, KC, TOK]) if want_f32 else None
        s, d = core.named_signal, core.named_dma_signal
        self.x_loaded = d("x_loaded")
        self.stats_ready = s("ln_stats_ready")
        self.mean_var_ready = s("ln_mean_var_ready")
        self.var_eps_ready = s("ln_var_eps_ready")
        self.rstd_ready = s("ln_rstd_ready")
        self.shift_ready = s("ln_shift_ready")
        self.h_ready = s("ln_h_ready")
        self.hT_in_psum = s("hT_in_psum")
        self.hT_hi_ready = s("hT_hi_ready")
        self.hT_lo_ready = s("hT_lo_ready")
        self.used = ["x_loaded", "ln_stats_ready", "ln_mean_var_ready", "ln_var_eps_ready", "ln_rstd_ready",
                     "ln_shift_ready", "ln_h_ready", "hT_in_psum", "hT_hi_ready", "hT_lo_ready"]

    def load(self, sp, g):
        after(sp, self.h_ready, g.back(2), apart=self.core)
        sp.dma_start(self.x[:, g.slot], tokens_of(self.x_dram, g)).then_inc(self.x_loaded[g.slot].sem, 16)

    def statistics(self, dve, g, first):
        nc, u = self.nc, g.slot
        if not first:
            self.variance(dve, g)
            return
        after_dma(dve, self.x_loaded, g)
        for p in range(PAIRS):
            last = nc.vector.bn_stats(self.stats[:, u, p, :], self.x[:, u, p, :])
        last.then_inc(self.stats_ready.sem, 1)

    def variance(self, dve, g):
        nc, u = self.nc, g.slot
        after(dve, self.stats_ready, g, apart=self.core)
        for p in range(PAIRS):
            last = nc.vector.bn_aggr(self.mean_var[:, u, p, :], self.stats[:, u, p, :])
        last.then_inc(self.mean_var_ready.sem, 1)
        after(dve, self.mean_var_ready, g)
        after(dve, self.rstd_ready, g.back(2))
        nc.vector.tensor_scalar(self.var_eps[:, u], self.mean_var[:, u, :, 1], LN_EPS, None,
                                ALU.add).then_inc(self.var_eps_ready.sem, 1)

    def root(self, pool, g):
        after(pool, self.var_eps_ready, g)
        after(pool, self.h_ready, g.back(2))
        self.nc.gpsimd.tensor_tensor(self.rstd[:, g.slot], self.var_eps[:, g.slot], self.core.minus_half[:, 0:PAIRS],
                                     ALU.pow).then_inc(self.rstd_ready.sem, 1)

    def shifts(self, dve, g):
        u = g.slot
        after(dve, self.rstd_ready, g)
        after(dve, self.h_ready, g.back(2))
        self.nc.vector.scalar_tensor_tensor(
            out=self.shift[:, u], in0=self.mean_var[:, u, :, 0], scalar=-1.0, in1=self.rstd[:, u],
            op0=ALU.mult, op1=ALU.mult).then_inc(self.shift_ready.sem, 1)

    def apply(self, act, g):
        u = g.slot
        after_dma(act, self.x_loaded, g)
        after(act, self.shift_ready, g)
        after(act, self.hT_in_psum, g.back(2))
        for p in range(PAIRS):
            last = self.nc.scalar.activation(self.h[:, u, p, :], self.x[:, u, p, :], ACT.Relu,
                                             bias=self.shift[:, u, p:p + 1], scale=self.rstd[:, u, p:p + 1])
        last.then_inc(self.h_ready.sem, 1)

    def transpose(self, pe, g, bank):
        after(pe, self.h_ready, g)
        for c in range(KC):
            for p in range(PAIRS):
                last = self.nc.tensor.transpose(self.core.ps[:, bank, c * TOK + p * P:c * TOK + (p + 1) * P],
                                                self.h[:, g.slot, p, c * P:(c + 1) * P], self.core.ident)
        last.then_inc(self.hT_in_psum.sem, 1)

    def evacuate_hi(self, act, g, bank):
        u = g.slot
        src = self.core.ps[:, bank, :].rearrange("p (c t) -> p c t", c=KC)
        after(act, self.hT_in_psum, g)
        if self.want_f32:
            self.nc.scalar.activation(self.hT[:, u], src, ACT.Copy)
        self.nc.scalar.activation(self.hT_hi[:, u], src, ACT.Copy).then_inc(self.hT_hi_ready.sem, 1)

    def evacuate_lo(self, dve, g, bank):
        u = g.slot
        after(dve, self.hT_hi_ready, g)
        self.nc.vector.tensor_tensor(self.hT_lo[:, u], self.core.ps[:, bank, :].rearrange("p (c t) -> p c t", c=KC),
                                     self.hT_hi[:, u], ALU.subtract).then_inc(self.hT_lo_ready.sem, 1)


def rows(w):
    return w.rearrange("(c p) n -> p c n", p=P)


def everywhere(b):
    return b.partition_broadcast(P)


def attention_layer(core, tag, x_dram, y_dram, adj, weights, biases, heads, static_mask):
    nc, ps, groups = core.nc, core.ps, core.groups
    HD = D // heads
    HPC = P // HD
    HH = heads // 2
    TP = BANK // (heads * S)
    NT = PAIRS // TP
    VW = HD + 1
    SCALE = float(HD) ** -0.5
    wq, wk, wv, wo = weights
    bq, bk, bv, bo = biases
    ctx = ExitStack()
    with ctx:
        sb = lambda n, shape, dt=F32: ctx.enter_context(nc.sbuf_tensor(f"{tag}_{n}", shape, dt))
        ln = LayerNorm(core, ctx, tag, x_dram)
        w_stage = sb("w_stage", [P, 4, KC, D])
        w_hi = sb("w_hi", [P, 4, KC, D], F32R)
        w_lo = sb("w_lo", [P, 4, KC, D], F32R)
        b_col = sb("b_col", [P, 3, KC])
        bo_row = sb("bo_row", [P, D])
        adj_u8 = sb("adj_u8", [P, 2, PAIRS, S], U8)
        allowed = sb("allowed", [P, 2, PAIRS, S])
        mask = sb("mask", [P, 2, PAIRS, S], BF16)
        q = sb("q", [P, 2, KC, TOK])
        k_bd = sb("k_bd", [P, 2, KC, NB, HPC, S])
        v_bd = sb("v_bd", [P, 2, PAIRS, 2, HH, 2, VW])
        shifted = sb("shifted", [P, 2, NT, TP * heads, S])
        prob = sb("prob", [P, 2, NT, TP * heads, S])
        smax = sb("smax", [P, 2, NT, TP * heads])
        probT = sb("probT", [P, 2, NT, TP * HH, P])
        rz = sb("rz", [P, 2, PAIRS, heads])
        o = sb("o", [P, 2, PAIRS, D])
        oT_hi = sb("oT_hi", [P, 2, KC, TOK], F32R)
        oT_lo = sb("oT_lo", [P, 2, KC, TOK], F32R)
        x_res = sb("x_res", [P, 2, PAIRS, D])
        x_bo = sb("x_bo", [P, 2, PAIRS, D])
        y = sb("y", [P, 2, PAIRS, D])

        s, d = core.named_signal, core.named_dma_signal
        x_res_loaded, adj_loaded, y_stored = d("x_res_loaded"), d("adj_loaded"), d("y_stored")
        allowed_ready = s("allowed_ready")
        mask_ready = s("mask_ready")
        q_in_psum, k_in_psum, v_in_psum = s("q_in_psum"), s("k_in_psum"), s("v_in_psum")
        q_ready = s("q_ready")
        k_bd_act_ready, k_bd_dve_ready = s("k_bd_act_ready"), s("k_bd_dve_ready")
        v_act_ready, v_dve_ready = s("v_act_ready"), s("v_dve_ready")
        sfx = f"_of_{NT}"
        scores_in_psum = s("scores_in_psum" + sfx, NT)
        smax_ready = s("smax_ready" + sfx, NT)
        shifted_ready = s("shifted_ready" + sfx, NT)
        prob_ready = s("prob_ready" + sfx, NT)
        probT_in_psum = s("probT_in_psum" + sfx, NT)
        probT_ready = s("probT_ready" + sfx, NT)
        o_in_psum, rz_ready, o_ready = s("o_in_psum"), s("rz_ready"), s("o_ready")
        oT_in_psum, oT_hi_ready, oT_lo_ready = s("oT_in_psum"), s("oT_hi_ready"), s("oT_lo_ready")
        proj_in_psum, x_bo_ready, y_ready = s("proj_in_psum"), s("x_bo_ready"), s("y_ready")
        used = ln.used + ["x_res_loaded", "adj_loaded", "y_stored", "mask_ready", "q_in_psum",
                          "k_in_psum", "v_in_psum", "q_ready", "k_bd_act_ready", "k_bd_dve_ready",
                          "v_act_ready", "v_dve_ready", "o_in_psum", "rz_ready", "o_ready", "oT_in_psum",
                          "oT_hi_ready", "oT_lo_ready", "proj_in_psum", "y_ready"]
        if static_mask is not None:
            used += ["allowed_ready"]
        if bo is not None:
            used += ["x_bo_ready"]
        used += [n + sfx for n in ("scores_in_psum", "smax_ready", "shifted_ready", "prob_ready",
                                   "probT_in_psum", "probT_ready")]
        B_HT = B_OT = 0
        B_Q, B_K, B_V, B_PROJ = 1, 2, 1, 3
        B_S, B_O = 4, 6
        B_PT = [4, 5] if NT == 2 else [5]
        w_loaded = core.once("setup_loaded_" + tag)
        hi_split = core.once("setup_hi_" + tag)
        lo_split = core.once("setup_lo_" + tag)
        made = core.once("setup_made_" + tag)
        MADE = 4
        n_loads = 4 + (3 if bq is not None else 0) + 1

        block = ctx.enter_context(nc.Block())

        @block.sync
        def _(sp):
            for n, w in enumerate((wq, wk, wv, wo)):
                sp.dma_start(w_stage[:, n], rows(w)).then_inc(w_loaded.sem, 16)
            if bq is not None:
                for n, b in enumerate((bq, bk, bv)):
                    sp.dma_start(b_col[:, n], b).then_inc(w_loaded.sem, 16)
            sp.dma_start(bo_row[:], everywhere(bo)).then_inc(w_loaded.sem, 16)

            def step(g):
                if g.exists(groups):
                    ln.load(sp, g)
                    after(sp, mask_ready, g.back(2), apart=core)
                    sp.dma_start(adj_u8[:, g.slot], adj[bass.ds(g.times(TOK), TOK), :]
                                 .rearrange("(p q) t -> q p t", q=P)).then_inc(adj_loaded[g.slot].sem, 16)
                r = g.back(2)
                if r.exists(groups):
                    after(sp, x_bo_ready, r.back(2), apart=core)
                    sp.dma_start(x_res[:, r.slot], tokens_of(x_dram, r)).then_inc(x_res_loaded[r.slot].sem, 16)
                e = g.back(3)
                if e.exists(groups):
                    after(sp, y_ready, e, apart=core)
                    sp.dma_start(tokens_of(y_dram, e), y[:, e.slot]).then_inc(y_stored[e.slot].sem, 16)

            run_steps(sp, step, groups, 3)
            for e in (groups - 2, groups - 1):
                after_dma(sp, y_stored, Group(None, e))

        @block.gpsimd
        def _(pool):
            nc.gpsimd.memset(k_bd[:], 0.0).then_inc(made.sem, 1)
            nc.gpsimd.memset(v_bd[:], 0.0).then_inc(made.sem, 1)
            pool.wait_ge(made.sem, 2)
            nc.gpsimd.memset(v_bd[0:S, :, :, :, :, 0, HD:VW], 1.0).then_inc(made.sem, 1)
            nc.gpsimd.memset(v_bd[S:P, :, :, :, :, 1, HD:VW], 1.0).then_inc(made.sem, 1)
            pool.wait_ge(w_loaded.sem, 16 * n_loads)
            core.wait_constants(pool)

            def step(g):
                if g.exists(groups):
                    ln.root(pool, g)
                    after_dma(pool, adj_loaded, g)
                    after(pool, scores_in_psum, g.back(2), apart=core)
                    if static_mask is None:
                        nc.gpsimd.tensor_scalar(mask[:, g.slot], adj_u8[:, g.slot], -1.0, MASKED,
                                                ALU.add, ALU.mult).then_inc(mask_ready.sem, 1)
                    else:
                        nc.gpsimd.tensor_scalar(allowed[:, g.slot], adj_u8[:, g.slot], -1.0, MASKED,
                                                ALU.add, ALU.mult).then_inc(allowed_ready.sem, 1)
                        after(pool, allowed_ready, g)
                        nc.gpsimd.tensor_tensor(mask[:, g.slot], allowed[:, g.slot],
                                                core.not_eye64[:].unsqueeze(1).to_broadcast([P, PAIRS, S]),
                                                ALU.mult).then_inc(mask_ready.sem, 1)
                r = g.back(2)
                if r.exists(groups):
                    after_dma(pool, x_res_loaded, r)
                    after(pool, y_ready, r.back(2))
                    nc.gpsimd.tensor_tensor(x_bo[:, r.slot], x_res[:, r.slot],
                                            bo_row[:].unsqueeze(1).to_broadcast([P, PAIRS, D]),
                                            ALU.add).then_inc(x_bo_ready.sem, 1)

            run_steps(pool, step, groups, 2)

        @block.scalar
        def _(act):
            act.wait_ge(w_loaded.sem, 16 * n_loads)
            for n in range(4):
                nc.scalar.activation(w_hi[:, n], w_stage[:, n], ACT.Copy).then_inc(hi_split.sem, 1)
            core.wait_constants(act)
            act.wait_ge(made.sem, MADE)

            def step(g):
                e = g.back(3)
                if e.exists(groups):
                    after(act, oT_in_psum, e)
                    after(act, proj_in_psum, e.back(2))
                    if bv is not None:
                        for c in range(KC):
                            last = nc.scalar.activation(oT_hi[:, e.slot, c], ps[:, B_OT, c * TOK:(c + 1) * TOK],
                                                        ACT.Identity, bias=b_col[:, 2, c:c + 1], scale=1.0)
                    else:
                        last = nc.scalar.activation(oT_hi[:, e.slot], ps[:, B_OT, :].rearrange("p (c t) -> p c t", c=KC),
                                                    ACT.Copy)
                    last.then_inc(oT_hi_ready.sem, 1)
                c2 = g.back(2)
                if c2.exists(groups):
                    for t in range(NT):
                        after(act, shifted_ready, c2, t + 1)
                        after(act, probT_in_psum, c2.back(2), t + 1)
                        nc.scalar.activation(prob[:, c2.slot, t], shifted[:, c2.slot, t], ACT.Exp,
                                             scale=SCALE).then_inc(prob_ready.sem, 1)
                b1 = g.back(1)
                if b1.exists(groups):
                    after(act, q_in_psum, b1)
                    after(act, scores_in_psum, b1.back(2))
                    if bq is not None:
                        for c in range(KC):
                            last = nc.scalar.activation(q[:, b1.slot, c], ps[:, B_Q, c * TOK:(c + 1) * TOK],
                                                        ACT.Identity, bias=b_col[:, 0, c:c + 1], scale=1.0)
                    else:
                        last = nc.scalar.activation(q[:, b1.slot], ps[:, B_Q, :].rearrange("p (c t) -> p c t", c=KC),
                                                    ACT.Copy)
                    last.then_inc(q_ready.sem, 1)
                if b1.exists(groups):
                    after(act, k_in_psum, b1)
                    for hp in range(HPC // 2):
                        r0 = hp * HD
                        for c in range(KC):
                            src = ps[r0:r0 + HD, B_K, c * TOK:(c + 1) * TOK].rearrange("p (b t) -> p b t", b=NB)
                            dst = k_bd[r0:r0 + HD, b1.slot, c, :, hp, :]
                            if bk is not None:
                                last = nc.scalar.activation(dst, src, ACT.Identity, bias=b_col[r0:r0 + HD, 1, c:c + 1],
                                                            scale=1.0)
                            else:
                                last = nc.scalar.activation(dst, src, ACT.Copy)
                    last.then_inc(k_bd_act_ready.sem, 1)
                if g.exists(groups):
                    ln.apply(act, g)
                if c2.exists(groups):
                    for t in range(NT):
                        after(act, probT_in_psum, c2, t + 1)
                        after(act, o_in_psum, c2.back(2))
                        nc.scalar.activation(probT[:, c2.slot, t], ps[:, B_PT[t], :].rearrange("p (j k) -> p j k", k=P),
                                             ACT.Copy).then_inc(probT_ready.sem, 1)
                if b1.exists(groups):
                    after(act, v_in_psum, b1)
                    after(act, o_in_psum, b1.back(2))
                    for par in range(2):
                        src = ps[0:S, B_V, :].rearrange("q (p j a e) -> q p j a e", p=PAIRS, j=HH, a=2)[:, :, :, par, :]
                        last = nc.scalar.activation(v_bd[par * S:(par + 1) * S, b1.slot, :, 0, :, par, 0:HD], src, ACT.Copy)
                    last.then_inc(v_act_ready.sem, 1)
                if g.exists(groups):
                    after(act, v_in_psum, g.back(2))
                    ln.evacuate_hi(act, g, B_HT)

            run_steps(act, step, groups, 3)

        @block.vector
        def _(dve):
            dve.wait_ge(w_loaded.sem, 16 * n_loads)
            for n in range(4):
                dve.wait_ge(hi_split.sem, n + 1)
                nc.vector.tensor_tensor(w_lo[:, n], w_stage[:, n], w_hi[:, n],
                                        ALU.subtract).then_inc(lo_split.sem, 1)
            core.wait_constants(dve)
            dve.wait_ge(made.sem, MADE)

            def step(g):
                c2, b1, e = g.back(2), g.back(1), g.back(3)

                def softmax_shift(t):
                    bank = ps[:, B_S + t, :].rearrange("p (h t) -> p h t", t=S)
                    after(dve, scores_in_psum, c2, t + 1)
                    nc.vector.reduce_max(smax[:, c2.slot, t], bank, AX.X).then_inc(smax_ready.sem, 1)
                    after(dve, smax_ready, c2, t + 1)
                    after(dve, prob_ready, c2.back(2), t + 1)
                    nc.vector.tensor_tensor(shifted[:, c2.slot, t], bank,
                                            smax[:, c2.slot, t].unsqueeze(2).to_broadcast([P, TP * heads, S]),
                                            ALU.subtract).then_inc(shifted_ready.sem, 1)

                if c2.exists(groups):
                    for t in range(NT):
                        softmax_shift(t)
                if e.exists(groups):
                    after(dve, oT_hi_ready, e)
                    after(dve, proj_in_psum, e.back(2))
                    if bv is not None:
                        for c in range(KC):
                            last = nc.vector.scalar_tensor_tensor(
                                out=oT_lo[:, e.slot, c], in0=ps[:, B_OT, c * TOK:(c + 1) * TOK],
                                scalar=b_col[:, 2, c:c + 1], in1=oT_hi[:, e.slot, c], op0=ALU.add, op1=ALU.subtract)
                    else:
                        last = nc.vector.tensor_tensor(oT_lo[:, e.slot], ps[:, B_OT, :].rearrange("p (c t) -> p c t", c=KC),
                                                       oT_hi[:, e.slot], ALU.subtract)
                    last.then_inc(oT_lo_ready.sem, 1)
                if g.exists(groups):
                    ln.statistics(dve, g, first=True)
                    ln.statistics(dve, g, first=False)
                if g.exists(groups):
                    ln.shifts(dve, g)
                if e.exists(groups):
                    after(dve, x_bo_ready, e)
                    after(dve, proj_in_psum, e)
                    after_dma(dve, y_stored, e.back(2))
                    nc.vector.tensor_tensor(y[:, e.slot], ps[:, B_PROJ, :].rearrange("q (p d) -> q p d", p=PAIRS),
                                            x_bo[:, e.slot], ALU.add).then_inc(y_ready.sem, 1)
                if b1.exists(groups):
                    after(dve, k_in_psum, b1)
                    after(dve, scores_in_psum, b1.back(2))
                    for hp in range(HPC // 2, HPC):
                        r0 = hp * HD
                        src = ps[r0:r0 + HD, B_K, :].rearrange("p (c b t) -> p c b t", c=KC, b=NB)
                        dst = k_bd[r0:r0 + HD, b1.slot, :, :, hp, :]
                        for c in range(KC):
                            if bk is not None:
                                last = nc.vector.tensor_scalar(dst[:, c], src[:, c], b_col[r0:r0 + HD, 1, c:c + 1], None, ALU.add)
                            else:
                                last = nc.vector.tensor_copy(dst[:, c], src[:, c])
                    last.then_inc(k_bd_dve_ready.sem, 1)
                    after(dve, v_in_psum, b1)
                    after(dve, o_in_psum, b1.back(2))
                    for par in range(2):
                        src = ps[S:P, B_V, :].rearrange("q (p j a e) -> q p j a e", p=PAIRS, j=HH, a=2)[:, :, :, par, :]
                        last = nc.vector.tensor_copy(v_bd[par * S:(par + 1) * S, b1.slot, :, 1, :, par, 0:HD], src)
                    last.then_inc(v_dve_ready.sem, 1)
                if NT == 1 and g.exists(groups):
                    after(dve, v_in_psum, g.back(2))
                    ln.evacuate_lo(dve, g, B_HT)
                if c2.exists(groups):
                    bank = ps[:, B_O:B_O + PAIRS, 0:heads * VW].rearrange("q p (h e) -> q p h e", h=heads)
                    after(dve, o_in_psum, c2)
                    nc.vector.reciprocal(rz[:, c2.slot], bank[:, :, :, HD]).then_inc(rz_ready.sem, 1)
                    after(dve, rz_ready, c2)
                    after(dve, oT_in_psum, c2.back(2))
                    for p in range(PAIRS):
                        last = nc.vector.tensor_tensor(
                            o[:, c2.slot, p].rearrange("q (h e) -> q h e", h=heads), bank[:, p, :, 0:HD],
                            rz[:, c2.slot, p].unsqueeze(2).to_broadcast([P, heads, HD]), ALU.mult)
                    last.then_inc(o_ready.sem, 1)
                if NT == 2 and g.exists(groups):
                    after(dve, v_in_psum, g.back(2))
                    ln.evacuate_lo(dve, g, B_HT)

            run_steps(dve, step, groups, 3)

        @block.tensor
        def _(pe):
            pe.wait_ge(lo_split.sem, 4)
            core.wait_constants(pe)
            pe.wait_ge(made.sem, MADE)
            ident_bf = core.ident_bf

            def weight(n):
                return (w_hi[:, n], w_lo[:, n])

            def project_T(n, src_hi, src_lo, bank):
                for oc in range(KC):
                    for c in range(KC):
                        last = mm3(nc, ps[:, bank, oc * TOK:(oc + 1) * TOK], weight(n), (src_hi, src_lo),
                                   c == 0, c == KC - 1,
                                   lambda w: w[:, c, oc * P:(oc + 1) * P], lambda a: a[:, c, :])
                return last

            def project(n, src_hi, src_lo, bank):
                for p in range(PAIRS):
                    for c in range(KC):
                        last = mm3(nc, ps[:, bank, p * D:(p + 1) * D], (src_hi, src_lo), weight(n),
                                   c == 0, c == KC - 1,
                                   lambda a: a[:, c, p * P:(p + 1) * P], lambda w: w[:, c, :])
                return last

            def step(g):
                c2, b1, e = g.back(2), g.back(1), g.back(3)
                if c2.exists(groups):
                    u = c2.slot
                    for t in range(NT):
                        if t == 0:
                            after(pe, mask_ready, c2)
                            after(pe, q_ready, c2)
                            after(pe, k_bd_act_ready, c2)
                            after(pe, k_bd_dve_ready, c2)
                        if NT == 2:
                            after(pe, probT_ready, c2.back(1), t + 1)
                        else:
                            after(pe, shifted_ready, c2.back(1))
                        if static_mask is not None:
                            nc.tensor.matmul(ps[:, B_S + t, 0:static_mask.shape[1]], ident_bf[:], static_mask[:],
                                             start=True, stop=False, skip_group_check=True)
                            w0 = static_mask.shape[1]
                            nc.tensor.matmul(ps[:, B_S + t, w0:BANK], ident_bf[:],
                                             mask[:, u, t].unsqueeze(1).to_broadcast([P, (BANK - w0) // S, S]),
                                             start=False, stop=False, skip_group_check=True)
                        else:
                            for pl in range(TP):
                                w0 = heads * S
                                nc.tensor.matmul(ps[:, B_S + t, pl * w0:(pl + 1) * w0], ident_bf[:],
                                                 mask[:, u, t * TP + pl].unsqueeze(1).to_broadcast([P, heads, S]),
                                                 start=pl == 0, stop=False, skip_group_check=True)
                        for pl in range(TP):
                            for b in range(2):
                                pb = (t * TP + pl) * 2 + b
                                for c in range(KC):
                                    col = pl * heads * S + c * HPC * S
                                    last = nc.tensor.matmul(
                                        ps[b * S:(b + 1) * S, B_S + t, col:col + HPC * S],
                                        q[:, u, c, pb * S:(pb + 1) * S], k_bd[:, u, c, pb],
                                        start=False, stop=True, skip_group_check=True)
                        last.then_inc(scores_in_psum.sem, 1)
                def transpose_o():
                    after(pe, o_ready, e)
                    after(pe, ln.hT_lo_ready, e.back(-2))
                    for c in range(KC):
                        for p in range(PAIRS):
                            last = nc.tensor.transpose(ps[:, B_OT, c * TOK + p * P:c * TOK + (p + 1) * P],
                                                       o[:, e.slot, p, c * P:(c + 1) * P], core.ident)
                    last.then_inc(oT_in_psum.sem, 1)

                def queries():
                    after(pe, ln.hT_hi_ready, b1)
                    after(pe, ln.hT_lo_ready, b1)
                    after(pe, v_act_ready, b1.back(1))
                    after(pe, v_dve_ready, b1.back(1))
                    project_T(0, ln.hT_hi[:, b1.slot], ln.hT_lo[:, b1.slot], B_Q).then_inc(q_in_psum.sem, 1)

                if NT == 1 and b1.exists(groups):
                    queries()
                if e.exists(groups):
                    transpose_o()
                if NT == 2 and b1.exists(groups):
                    queries()
                if b1.exists(groups):
                    after(pe, k_bd_act_ready, b1.back(1))
                    after(pe, k_bd_dve_ready, b1.back(1))
                    project_T(1, ln.hT_hi[:, b1.slot], ln.hT_lo[:, b1.slot], B_K).then_inc(k_in_psum.sem, 1)
                if e.exists(groups):
                    after(pe, oT_hi_ready, e)
                    after(pe, oT_lo_ready, e)
                    after(pe, y_ready, e.back(1))
                    project(3, oT_hi[:, e.slot], oT_lo[:, e.slot], B_PROJ).then_inc(proj_in_psum.sem, 1)
                if c2.exists(groups):
                    u = c2.slot
                    for t in range(NT):
                        after(pe, prob_ready, c2, t + 1)
                        if NT == 1:
                            after(pe, probT_ready, c2.back(1), 1)
                        pr = prob[:, u, t].rearrange("p h t -> p (h t)")
                        for j in range(TP * HH):
                            last = nc.tensor.transpose(ps[:, B_PT[t], j * P:(j + 1) * P], pr[:, j * P:(j + 1) * P],
                                                       core.ident)
                        last.then_inc(probT_in_psum.sem, 1)
                if b1.exists(groups):
                    after(pe, q_ready, b1)
                    project(2, ln.hT_hi[:, b1.slot], ln.hT_lo[:, b1.slot], B_V).then_inc(v_in_psum.sem, 1)
                if g.exists(groups):
                    after(pe, oT_lo_ready, g.back(3))
                    ln.transpose(pe, g, B_HT)
                if c2.exists(groups):
                    u = c2.slot
                    after(pe, probT_ready, c2)
                    after(pe, v_act_ready, c2)
                    after(pe, v_dve_ready, c2)
                    after(pe, o_ready, c2.back(1))
                    for p in range(PAIRS):
                        for b in range(2):
                            for j in range(HH):
                                last = nc.tensor.matmul(
                                    ps[b * S:(b + 1) * S, B_O + p, j * 2 * VW:(j + 1) * 2 * VW],
                                    probT[:, u, p // TP, (p % TP) * HH + j, b * S:(b + 1) * S],
                                    v_bd[:, u, p, b, j], start=True, stop=True, skip_group_check=True)
                    last.then_inc(o_in_psum.sem, 1)

            run_steps(pe, step, groups, 3)
    core.end_layer(used)


def static_masks():
    sq = np.arange(S)
    r, f = sq // 8, sq % 8
    dr, df = np.abs(r[:, None] - r[None, :]), np.abs(f[:, None] - f[None, :])
    masks = np.stack([df == 0, dr == 0, r[:, None] - f[:, None] == r[None, :] - f[None, :],
                      r[:, None] + f[:, None] == r[None, :] + f[None, :],
                      (dr == 2) & (df == 1) | (dr == 1) & (df == 2) | np.eye(S, dtype=bool),
                      (dr <= 1) & (df <= 1)])
    bias = np.where(masks, 0.0, -MASKED).astype(np.float32)
    return np.tile(bias.transpose(1, 0, 2).reshape(S, -1), (2, 1))


def constants():
    eye = np.eye(S, dtype=np.float32)
    eye64 = np.tile(eye, (2, 1))
    same = np.kron(np.eye(2, dtype=np.float32), np.ones((S, S), np.float32))
    return np.ascontiguousarray(np.concatenate(
        [np.eye(P, dtype=np.float32), eye64, 1.0 - eye64, same, static_masks()], axis=1))


def load_constants(core, ctx, const):
    nc = core.nc
    n = const.shape[1]
    ns = n - 3 * P
    c = ctx.enter_context(nc.sbuf_tensor("constants_sb", [P, n], F32))
    core.ident_bf = ctx.enter_context(nc.sbuf_tensor("ident_bf", [P, P], BF16))
    core.static_mask = ctx.enter_context(nc.sbuf_tensor("static_mask", [P, ns], BF16))
    core.minus_half = ctx.enter_context(nc.sbuf_tensor("minus_half", [P, 16], F32))
    core.ident = c[:, 0:P]
    core.eye64 = c[:, P:P + S]
    core.not_eye64 = c[:, P + S:2 * P]
    core.same_batch = c[:, 2 * P:3 * P]
    loaded = core.once("constants_loaded")
    core.waits_passed = core.once("waits_passed")
    core.constants_ready = core.once("constants_ready")
    with nc.Block() as block:

        @block.sync
        def _(sp):
            sp.dma_start(c[:], const).then_inc(loaded.sem, 16)

        @block.vector
        def _(dve):
            dve.wait_ge(loaded.sem, 16)
            nc.vector.memset(core.minus_half[:], -0.5)
            nc.vector.tensor_copy(core.ident_bf[:], c[:, 0:P])
            nc.vector.tensor_copy(core.static_mask[:], c[:, 3 * P:n]).then_inc(core.constants_ready.sem, 1)


def gated_graph_layer(core, x_dram, y_dram, adj, w, b):
    nc, ps, groups = core.nc, core.ps, core.groups
    heads, HD = 8, D // 8
    HPC, HH = P // HD, heads // 2
    VW = HD + 1
    NT = PAIRS
    SCALE = float(HD) ** -0.5
    THRESHOLD = 0.1
    ctx = ExitStack()
    with ctx:
        sb = lambda n, shape, dt=F32: ctx.enter_context(nc.sbuf_tensor(f"l3_{n}", shape, dt))
        ln = LayerNorm(core, ctx, "l3", x_dram)
        w_stage = sb("w_stage", [P, 5, KC, D])
        block_w = sb("block_w", [P, P])
        w_hi = sb("w_hi", [P, 4, KC, D], F32R)
        w_lo = sb("w_lo", [P, 4, KC, D], F32R)
        b_col = sb("b_col", [P, 4, KC])
        qk_bias = sb("qk_bias", [P, 2, KC])
        m_bias = sb("m_bias", [P, D])
        sem_bias = sb("sem_bias", [P, D])
        adj_u8 = sb("adj_u8", [P, 2, PAIRS, S], U8)
        mask = sb("mask", [P, 2, PAIRS, S], BF16)
        keep = sb("keep", [P, 2, PAIRS])
        q = sb("q", [P, 2, KC, TOK])
        k_bd = sb("k_bd", [P, 2, KC, NB, HPC, S])
        n_bd = sb("n_bd", [P, 2, KC, NB, HPC, S])
        nT = sb("nT", [P, 2, KC, TOK])
        v_bd = sb("v_bd", [P, 2, PAIRS, 2, HH, 2, VW])
        m = sb("m", [P, 2, PAIRS * heads, HD])
        m_sq = sb("m_sq", [P, 2, PAIRS * heads, HD])
        n = sb("n", [P, 2, PAIRS * heads, HD])
        norm_sq = sb("norm_sq", [P, 2, PAIRS * heads])
        norm_cl = sb("norm_cl", [P, 2, PAIRS * heads])
        r_norm = sb("r_norm", [P, 2, PAIRS * heads])
        shifted = sb("shifted", [P, 2, NT, heads, S])
        prob = sb("prob", [P, 2, NT, heads, S])
        linked = sb("linked", [P, 2, NT, heads, S])
        smax = sb("smax", [P, 2, NT, heads])
        z = sb("z", [P, 2, NT, heads])
        rz = sb("rz", [P, 2, NT, heads])
        kz = sb("kz", [P, 2, NT, heads])
        kzs = sb("kzs", [P, 2, NT, heads])
        den = sb("den", [P, 2, NT, heads])
        r_den = sb("r_den", [P, 2, NT, heads])
        factor = sb("factor", [P, 2, NT, heads])
        linkedT = sb("linkedT", [P, 2, NT, HH, P])
        t = sb("t", [P, 2, PAIRS, D])
        x_res = sb("x_res", [P, 2, PAIRS, D])
        y = sb("y", [P, 2, PAIRS, D])

        s, d = core.named_signal, core.named_dma_signal
        x_res_loaded, adj_loaded, y_stored = d("x_res_loaded"), d("adj_loaded"), d("y_stored")
        mask_ready, keep_ready = s("mask_ready"), s("keep_ready")
        q_in_psum, k_in_psum, sem_in_psum, m_in_psum = s("q_in_psum"), s("k_in_psum"), s("v_in_psum"), s("m_in_psum")
        q_ready, m_ready, m_sq_ready = s("q_ready"), s("m_ready"), s("m_sq_ready")
        norm_sq_ready, norm_cl_ready, r_norm_ready = s("norm_sq_ready"), s("norm_cl_ready"), s("r_norm_ready")
        n_ready, nT_in_psum, nT_ready = s("n_ready"), s("nT_in_psum"), s("nT_ready")
        n_bd_ready = s("n_bd_ready")
        k_bd_ready = s("k_bd_act_ready")
        sem_ready = s("v_dve_ready")
        scores_in_psum = s("scores_in_psum_of_2", 2)
        smax_ready = s("smax_ready_of_2", 2)
        shifted_ready = s("shifted_ready_of_2", 2)
        prob_ready = s("prob_ready_of_2", 2)
        z_ready = s("z_ready", 2)
        cos_in_psum = s("cos_in_psum", 2)
        linked_ready = s("linked_ready", 2)
        linkedT_in_psum = s("probT_in_psum_of_2", 2)
        linkedT_ready = s("probT_ready_of_2", 2)
        kz_steps, factor_steps = s("kz_steps", 2), s("factor_steps", 4)
        o_in_psum, t_ready, y_ready = s("o_in_psum"), s("o_ready"), s("y_ready")
        used = ln.used + ["x_res_loaded", "adj_loaded", "y_stored", "mask_ready", "keep_ready", "q_in_psum", "k_in_psum",
                          "v_in_psum", "m_in_psum", "q_ready", "m_ready", "m_sq_ready", "norm_sq_ready", "norm_cl_ready",
                          "r_norm_ready", "n_ready", "nT_in_psum", "nT_ready", "n_bd_ready", "k_bd_act_ready",
                          "v_dve_ready", "scores_in_psum_of_2", "smax_ready_of_2", "shifted_ready_of_2",
                          "prob_ready_of_2", "z_ready", "cos_in_psum", "linked_ready", "probT_in_psum_of_2",
                          "probT_ready_of_2", "o_in_psum", "kz_steps", "factor_steps", "o_ready", "y_ready"]
        B_HT, B_Q, B_M, B_K, B_SEM, B_S, B_COS, B_O = 0, 1, 2, 1, 2, 3, 5, 6
        w_loaded = core.once("setup_loaded_l3")
        zeroed = core.once("setup_zeroed_l3")
        folded = core.once("setup_folded_l3")
        hi_split = core.once("setup_hi_l3")
        preset = core.once("setup_preset_l3")
        made = core.once("setup_made_l3")
        PRESET, MADE = 5, 6
        W_MAP, W_QT, W_KT, W_MAPT, W_GMAP = range(5)

        block = ctx.enter_context(nc.Block())

        @block.sync
        def _(sp):
            for i, name in enumerate(("map", "qT", "kT", "mapT", "gmap")):
                sp.dma_start(w_stage[:, i], rows(w[name])).then_inc(w_loaded.sem, 16)
            for i, name in enumerate(("map", "q", "k", "gmap")):
                sp.dma_start(b_col[:, i], b[name]).then_inc(w_loaded.sem, 16)
            sp.dma_start(m_bias[:], everywhere(b["map_row"])).then_inc(w_loaded.sem, 16)
            sp.wait_ge(zeroed.sem, 1)
            for i in range(HPC):
                sp.dma_start(block_w[i * HD:(i + 1) * HD, i * HD:(i + 1) * HD], w["gcn_WT"]).then_inc(w_loaded.sem, 16)

            def step(g):
                if g.exists(groups):
                    ln.load(sp, g)
                    after(sp, mask_ready, g.back(2), apart=core)
                    after(sp, keep_ready, g.back(2), apart=core)
                    sp.dma_start(adj_u8[:, g.slot], adj[bass.ds(g.times(TOK), TOK), :]
                                 .rearrange("(p q) t -> q p t", q=P)).then_inc(adj_loaded[g.slot].sem, 16)
                r = g.back(2)
                if r.exists(groups):
                    after(sp, y_ready, r.back(2), apart=core)
                    sp.dma_start(x_res[:, r.slot], tokens_of(x_dram, r)).then_inc(x_res_loaded[r.slot].sem, 16)
                e = g.back(3)
                if e.exists(groups):
                    after(sp, y_ready, e, apart=core)
                    sp.dma_start(tokens_of(y_dram, e), y[:, e.slot]).then_inc(y_stored[e.slot].sem, 16)

            run_steps(sp, step, groups, 3)
            for e in (groups - 2, groups - 1):
                after_dma(sp, y_stored, Group(None, e))

        @block.gpsimd
        def _(pool):
            nc.gpsimd.memset(block_w[:], 0.0).then_inc(zeroed.sem, 1)
            nc.gpsimd.memset(k_bd[:], 0.0).then_inc(preset.sem, 1)
            nc.gpsimd.memset(n_bd[:], 0.0).then_inc(preset.sem, 1)
            nc.gpsimd.memset(v_bd[:], 0.0).then_inc(preset.sem, 1)
            pool.wait_ge(preset.sem, 3)
            nc.gpsimd.memset(v_bd[0:S, :, :, :, :, 0, HD:VW], 1.0).then_inc(preset.sem, 1)
            nc.gpsimd.memset(v_bd[S:P, :, :, :, :, 1, HD:VW], 1.0).then_inc(preset.sem, 1)
            core.wait_constants(pool)

            def step(g):
                if g.exists(groups):
                    ln.root(pool, g)
                b1 = g.back(1)
                if b1.exists(groups):
                    u = b1.slot
                    after(pool, norm_cl_ready, b1)
                    after(pool, n_ready, b1.back(2))
                    nc.gpsimd.tensor_tensor(r_norm[:, u], norm_cl[:, u], core.minus_half[:, 0:PAIRS * heads],
                                            ALU.pow).then_inc(r_norm_ready.sem, 1)
                    after(pool, r_norm_ready, b1)
                    after(pool, nT_in_psum, b1.back(2))
                    nc.gpsimd.tensor_tensor(n[:, u], m[:, u], r_norm[:, u].unsqueeze(2).to_broadcast([P, PAIRS * heads, HD]),
                                            ALU.mult).then_inc(n_ready.sem, 1)

            run_steps(pool, step, groups, 1)

        @block.scalar
        def _(act):
            act.wait_ge(folded.sem, 1)
            for i, bank in ((0, 0), (1, 1), (3, 2)):
                nc.scalar.activation(w_hi[:, i], ps[:, bank, :].rearrange("p (c n) -> p c n", c=KC),
                                     ACT.Copy).then_inc(hi_split.sem, 1)
            nc.scalar.activation(w_hi[:, 2], w_stage[:, W_MAPT], ACT.Copy).then_inc(hi_split.sem, 1)
            core.wait_constants(act)
            act.wait_ge(preset.sem, PRESET)
            act.wait_ge(made.sem, MADE)

            def step(g):
                c2, b1 = g.back(2), g.back(1)

                def exponentials(i):
                    after(act, shifted_ready, c2, i + 1)
                    after(act, linked_ready, c2.back(2), i + 1)
                    after(act, z_ready, c2.back(2), i + 1)
                    nc.scalar.activation(prob[:, c2.slot, i], shifted[:, c2.slot, i], ACT.Exp,
                                         scale=SCALE).then_inc(prob_ready.sem, 1)

                def evacuate_linkedT(i):
                    after(act, linkedT_in_psum, c2, i + 1)
                    after(act, o_in_psum, c2.back(2))
                    nc.scalar.activation(linkedT[:, c2.slot, i], ps[:, B_S + i, :].rearrange("p (j k) -> p j k", k=P),
                                         ACT.Copy).then_inc(linkedT_ready.sem, 1)

                if c2.exists(groups):
                    exponentials(0)
                if b1.exists(groups):
                    u = b1.slot
                    after(act, q_in_psum, b1)
                    after(act, scores_in_psum, b1.back(2))
                    for c in range(KC):
                        last = nc.scalar.activation(q[:, u, c], ps[:, B_Q, c * TOK:(c + 1) * TOK], ACT.Identity,
                                                    bias=qk_bias[:, 0, c:c + 1], scale=1.0)
                    last.then_inc(q_ready.sem, 1)
                if c2.exists(groups):
                    exponentials(1)
                    after(act, nT_ready, c2)
                    after(act, cos_in_psum, c2.back(2))
                    for hp in range(HPC):
                        r0 = hp * HD
                        last = nc.scalar.activation(
                            n_bd[r0:r0 + HD, c2.slot, :, :, hp, :],
                            nT[r0:r0 + HD, c2.slot].rearrange("p c (b t) -> p c b t", b=NB), ACT.Copy)
                    last.then_inc(n_bd_ready.sem, 1)
                if b1.exists(groups):
                    after(act, m_ready, b1)
                    after(act, norm_sq_ready, b1.back(2))
                    nc.scalar.activation(m_sq[:, b1.slot], m[:, b1.slot], ACT.Square).then_inc(m_sq_ready.sem, 1)
                if g.exists(groups):
                    ln.apply(act, g)
                if b1.exists(groups):
                    after(act, k_in_psum, b1)
                    for hp in range(HPC):
                        r0 = hp * HD
                        for c in range(KC):
                            last = nc.scalar.activation(
                                k_bd[r0:r0 + HD, b1.slot, c, :, hp, :],
                                ps[r0:r0 + HD, B_K, c * TOK:(c + 1) * TOK].rearrange("p (b t) -> p b t", b=NB),
                                ACT.Identity, bias=qk_bias[r0:r0 + HD, 1, c:c + 1], scale=1.0)
                    last.then_inc(k_bd_ready.sem, 1)
                if c2.exists(groups):
                    evacuate_linkedT(0)
                if g.exists(groups):
                    after(act, sem_in_psum, g.back(2))
                    ln.evacuate_hi(act, g, B_HT)
                if c2.exists(groups):
                    evacuate_linkedT(1)

            run_steps(act, step, groups, 2)

        @block.vector
        def _(dve):
            dve.wait_ge(folded.sem, 1)
            for j, (i, bank) in enumerate(((0, 0), (1, 1), (3, 2))):
                dve.wait_ge(hi_split.sem, j + 1)
                nc.vector.tensor_tensor(w_lo[:, i], ps[:, bank, :].rearrange("p (c n) -> p c n", c=KC), w_hi[:, i],
                                        ALU.subtract).then_inc(made.sem, 1)
            dve.wait_ge(hi_split.sem, 4)
            nc.vector.tensor_tensor(w_lo[:, 2], w_stage[:, W_MAPT], w_hi[:, 2], ALU.subtract).then_inc(made.sem, 1)
            nc.vector.tensor_tensor(qk_bias[:], ps[:, 3, 0:2 * KC].rearrange("p (a c) -> p a c", a=2), b_col[:, 1:3],
                                    ALU.add).then_inc(made.sem, 1)
            nc.vector.tensor_copy(sem_bias[:], ps[:, 4, 0:D]).then_inc(made.sem, 1)
            core.wait_constants(dve)
            dve.wait_ge(preset.sem, PRESET)
            dve.wait_ge(made.sem, MADE)

            def step(g):
                c2, b1, e = g.back(2), g.back(1), g.back(3)

                def softmax_shift(i):
                    u = c2.slot
                    bank = ps[:, B_S + i, :].rearrange("p (h t) -> p h t", t=S)
                    after(dve, scores_in_psum, c2, i + 1)
                    nc.vector.reduce_max(smax[:, u, i], bank, AX.X).then_inc(smax_ready.sem, 1)
                    after(dve, smax_ready, c2, i + 1)
                    after(dve, prob_ready, c2.back(2), i + 1)
                    nc.vector.tensor_tensor(shifted[:, u, i], bank,
                                            smax[:, u, i].unsqueeze(2).to_broadcast([P, heads, S]),
                                            ALU.subtract).then_inc(shifted_ready.sem, 1)

                def link(i):
                    u = c2.slot
                    after(dve, prob_ready, c2, i + 1)
                    after(dve, cos_in_psum, c2, i + 1)
                    after(dve, linkedT_in_psum, c2.back(2), i + 1)
                    nc.vector.scalar_tensor_tensor(
                        out=linked[:, u, i], in0=ps[:, B_COS, :].rearrange("p (h t) -> p h t", t=S), scalar=THRESHOLD,
                        in1=prob[:, u, i], op0=ALU.is_gt, op1=ALU.mult).then_inc(linked_ready.sem, 1)

                if c2.exists(groups):
                    softmax_shift(0)
                if g.exists(groups):
                    ln.statistics(dve, g, first=True)
                if e.exists(groups):
                    u = e.slot
                    bank = ps[:, B_O:B_O + PAIRS, 0:heads * VW].rearrange("q p (h e) -> q p h e", h=heads)
                    after(dve, kz_steps, e)
                    after(dve, o_in_psum, e)
                    nc.vector.tensor_tensor(kzs[:, u], bank[:, :, :, HD], kz[:, u], ALU.mult).then_inc(factor_steps.sem, 1)
                    after(dve, factor_steps, e, 1)
                    nc.vector.tensor_scalar(den[:, u], kzs[:, u], 1.0, None, ALU.add).then_inc(factor_steps.sem, 1)
                    after(dve, factor_steps, e, 2)
                    nc.vector.reciprocal(r_den[:, u], den[:, u]).then_inc(factor_steps.sem, 1)
                    after(dve, factor_steps, e, 3)
                    nc.vector.tensor_tensor(factor[:, u], kz[:, u], r_den[:, u], ALU.mult).then_inc(factor_steps.sem, 1)
                    after(dve, factor_steps, e)
                    for p in range(PAIRS):
                        last = nc.vector.tensor_tensor(
                            t[:, u, p].rearrange("q (h e) -> q h e", h=heads), bank[:, p, :, 0:HD],
                            factor[:, u, p].unsqueeze(2).to_broadcast([P, heads, HD]), ALU.mult)
                    last.then_inc(t_ready.sem, 1)
                if c2.exists(groups):
                    softmax_shift(1)
                    after(dve, nT_in_psum, c2)
                    after(dve, cos_in_psum, c2.back(2))
                    after(dve, n_bd_ready, c2.back(2))
                    nc.vector.tensor_copy(nT[:, c2.slot], ps[:, B_HT, :].rearrange("p (c t) -> p c t", c=KC)).then_inc(
                        nT_ready.sem, 1)
                if g.exists(groups):
                    ln.statistics(dve, g, first=False)
                    after_dma(dve, adj_loaded, g)
                    after(dve, scores_in_psum, g.back(2))
                    nc.vector.tensor_scalar(mask[:, g.slot], adj_u8[:, g.slot], -MASKED, None,
                                            ALU.mult).then_inc(mask_ready.sem, 1)
                if b1.exists(groups):
                    after(dve, m_in_psum, b1)
                    after(dve, n_ready, b1.back(2))
                    nc.vector.tensor_tensor(m[:, b1.slot].rearrange("q (p h) e -> q p (h e)", p=PAIRS),
                                            ps[:, B_M, :].rearrange("q (p n) -> q p n", p=PAIRS),
                                            m_bias[:].unsqueeze(1).to_broadcast([P, PAIRS, D]), ALU.add).then_inc(m_ready.sem, 1)
                if e.exists(groups):
                    after(dve, t_ready, e)
                    after_dma(dve, x_res_loaded, e)
                    after_dma(dve, y_stored, e.back(2))
                    nc.vector.scalar_tensor_tensor(out=y[:, e.slot], in0=t[:, e.slot], scalar=0.0, in1=x_res[:, e.slot],
                                                   op0=ALU.max, op1=ALU.add).then_inc(y_ready.sem, 1)
                if g.exists(groups):
                    ln.shifts(dve, g)
                if c2.exists(groups):
                    for i in range(NT):
                        after(dve, prob_ready, c2, i + 1)
                        after(dve, kz_steps, c2.back(2))
                        nc.vector.reduce_sum(z[:, c2.slot, i], prob[:, c2.slot, i], AX.X).then_inc(z_ready.sem, 1)
                if b1.exists(groups):
                    u = b1.slot
                    after(dve, m_sq_ready, b1)
                    nc.vector.reduce_sum(norm_sq[:, u], m_sq[:, u], AX.X).then_inc(norm_sq_ready.sem, 1)
                if c2.exists(groups):
                    link(0)
                if b1.exists(groups):
                    u = b1.slot
                    after(dve, norm_sq_ready, b1)
                    after(dve, r_norm_ready, b1.back(2))
                    nc.vector.tensor_scalar(norm_cl[:, u], norm_sq[:, u], 1e-16, None, ALU.max).then_inc(norm_cl_ready.sem, 1)
                if c2.exists(groups):
                    u = c2.slot
                    after(dve, z_ready, c2)
                    nc.vector.reciprocal(rz[:, u], z[:, u]).then_inc(kz_steps.sem, 1)
                if b1.exists(groups):
                    u = b1.slot
                    after(dve, sem_in_psum, b1)
                    after(dve, o_in_psum, b1.back(2))
                    for bb in range(2):
                        for par in range(2):
                            def of_parity(ap):
                                return ap.rearrange("q p (j a e) -> q p j a e", j=HH, a=2)[:, :, :, par, :]
                            r0 = bb * S
                            last = nc.vector.tensor_tensor(
                                v_bd[par * S:(par + 1) * S, u, :, bb, :, par, 0:HD],
                                of_parity(ps[r0:r0 + S, B_SEM, :].rearrange("q (p n) -> q p n", p=PAIRS)),
                                of_parity(sem_bias[r0:r0 + S].unsqueeze(1).to_broadcast([S, PAIRS, D])), ALU.add)
                    last.then_inc(sem_ready.sem, 1)
                if c2.exists(groups):
                    u = c2.slot
                    link(1)
                    after(dve, kz_steps, c2, 1)
                    after(dve, keep_ready, c2)
                    after(dve, factor_steps, c2.back(2))
                    nc.vector.tensor_tensor(kz[:, u], rz[:, u], keep[:, u].unsqueeze(2).to_broadcast([P, NT, heads]),
                                            ALU.mult).then_inc(kz_steps.sem, 1)
                if g.exists(groups):
                    after(dve, kz_steps, g.back(2))
                    nc.vector.tensor_scalar(keep[:, g.slot], adj_u8[:, g.slot, :, 0], -1.0, 1.0, ALU.mult,
                                            ALU.add).then_inc(keep_ready.sem, 1)
                    after(dve, sem_in_psum, g.back(2))
                    ln.evacuate_lo(dve, g, B_HT)

            run_steps(dve, step, groups, 3)

        @block.tensor
        def _(pe):
            pe.wait_ge(w_loaded.sem, 16 * (10 + HPC))
            for i, wt in ((0, W_QT), (1, W_KT)):
                for jc in range(KC):
                    for c in range(KC):
                        nc.tensor.matmul(ps[:, i, jc * D:(jc + 1) * D], w_stage[:, W_MAP, c, jc * P:(jc + 1) * P],
                                         w_stage[:, wt, c, :], start=c == 0, stop=c == KC - 1)
                for oc in range(KC):
                    for c in range(KC):
                        nc.tensor.matmul(ps[:, 3, i * KC + oc:i * KC + oc + 1], w_stage[:, wt, c, oc * P:(oc + 1) * P],
                                         b_col[:, 0, c:c + 1], start=c == 0, stop=c == KC - 1)
            for jc in range(KC):
                for c in range(KC):
                    nc.tensor.matmul(ps[:, 2, jc * D + c * P:jc * D + (c + 1) * P],
                                     w_stage[:, W_GMAP, c, jc * P:(jc + 1) * P], block_w[:], start=True, stop=True)
            for c in range(KC):
                last = nc.tensor.matmul(ps[:, 4, c * P:(c + 1) * P], b_col[:, 3, c:c + 1].to_broadcast([P, P]), block_w[:],
                                        start=True, stop=True)
            last.then_inc(folded.sem, 1)
            core.wait_constants(pe)
            pe.wait_ge(preset.sem, PRESET)
            pe.wait_ge(made.sem, MADE)

            def weight(i):
                return (w_hi[:, i], w_lo[:, i])

            def project_T(i, g, bank):
                for oc in range(KC):
                    for c in range(KC):
                        last = mm3(nc, ps[:, bank, oc * TOK:(oc + 1) * TOK], weight(i), (ln.hT_hi[:, g.slot], ln.hT_lo[:, g.slot]),
                                   c == 0, c == KC - 1, lambda a: a[:, c, oc * P:(oc + 1) * P], lambda a: a[:, c, :])
                return last

            def project(i, g, bank):
                for p in range(PAIRS):
                    for c in range(KC):
                        last = mm3(nc, ps[:, bank, p * D:(p + 1) * D], (ln.hT_hi[:, g.slot], ln.hT_lo[:, g.slot]), weight(i),
                                   c == 0, c == KC - 1, lambda a: a[:, c, p * P:(p + 1) * P], lambda a: a[:, c, :])
                return last

            def by_head(i, bank, stationary, moving, start, u):
                for bb in range(2):
                    pb = 2 * i + bb
                    for c in range(KC):
                        last = nc.tensor.matmul(ps[bb * S:(bb + 1) * S, bank, c * HPC * S:(c + 1) * HPC * S],
                                                stationary[:, u, c, pb * S:(pb + 1) * S], moving[:, u, c, pb],
                                                start=start and c == 0, stop=True, skip_group_check=True)
                return last

            def cosines(c2, i):
                after(pe, nT_ready, c2)
                after(pe, n_bd_ready, c2)
                if i == 0:
                    after(pe, linked_ready, c2.back(1))
                else:
                    after(pe, linked_ready, c2, 1)
                by_head(i, B_COS, nT, n_bd, True, c2.slot).then_inc(cos_in_psum.sem, 1)

            def transpose_linked(c2, i):
                after(pe, linked_ready, c2, i + 1)
                li = linked[:, c2.slot, i].rearrange("p h t -> p (h t)")
                for j in range(HH):
                    last = nc.tensor.transpose(ps[:, B_S + i, j * P:(j + 1) * P], li[:, j * P:(j + 1) * P], core.ident)
                last.then_inc(linkedT_in_psum.sem, 1)

            def scores(c2, i):
                after(pe, mask_ready, c2)
                after(pe, q_ready, c2)
                after(pe, k_bd_ready, c2)
                after(pe, linkedT_ready, c2.back(1), i + 1)
                nc.tensor.matmul(ps[:, B_S + i, :], core.ident_bf[:],
                                 mask[:, c2.slot, i].unsqueeze(1).to_broadcast([P, heads, S]),
                                 start=True, stop=False, skip_group_check=True)
                by_head(i, B_S + i, q, k_bd, False, c2.slot).then_inc(scores_in_psum.sem, 1)

            def step(g):
                c2, b1, e = g.back(2), g.back(1), g.back(3)
                if c2.exists(groups):
                    scores(c2, 0)
                if e.exists(groups):
                    u = e.slot
                    after(pe, linkedT_ready, e)
                    after(pe, sem_ready, e)
                    after(pe, t_ready, e.back(1))
                    for p in range(PAIRS):
                        for bb in range(2):
                            for j in range(HH):
                                last = nc.tensor.matmul(ps[bb * S:(bb + 1) * S, B_O + p, j * 2 * VW:(j + 1) * 2 * VW],
                                                        linkedT[:, u, p, j, bb * S:(bb + 1) * S], v_bd[:, u, p, bb, j],
                                                        start=True, stop=True, skip_group_check=True)
                    last.then_inc(o_in_psum.sem, 1)
                if c2.exists(groups):
                    scores(c2, 1)
                if b1.exists(groups):
                    after(pe, ln.hT_hi_ready, b1)
                    after(pe, ln.hT_lo_ready, b1)
                    after(pe, k_bd_ready, b1.back(1))
                    project_T(0, b1, B_Q).then_inc(q_in_psum.sem, 1)
                if c2.exists(groups):
                    after(pe, n_ready, c2)
                    after(pe, ln.hT_lo_ready, c2.back(-1))
                    nn = n[:, c2.slot].rearrange("q (p h) e -> q p (h e)", p=PAIRS)
                    for c in range(KC):
                        for p in range(PAIRS):
                            last = nc.tensor.transpose(ps[:, B_HT, c * TOK + p * P:c * TOK + (p + 1) * P],
                                                       nn[:, p, c * P:(c + 1) * P], core.ident)
                    last.then_inc(nT_in_psum.sem, 1)
                if b1.exists(groups):
                    after(pe, sem_ready, b1.back(1))
                    project(2, b1, B_M).then_inc(m_in_psum.sem, 1)
                    after(pe, q_ready, b1)
                    project_T(1, b1, B_K).then_inc(k_in_psum.sem, 1)
                    after(pe, m_ready, b1)
                    project(3, b1, B_SEM).then_inc(sem_in_psum.sem, 1)
                if c2.exists(groups):
                    cosines(c2, 0)
                    cosines(c2, 1)
                    transpose_linked(c2, 0)
                if g.exists(groups):
                    after(pe, ln.h_ready, g)
                    after(pe, nT_ready, g.back(2))
                    ln.transpose(pe, g, B_HT)
                if c2.exists(groups):
                    transpose_linked(c2, 1)

            run_steps(pe, step, groups, 3)
    core.end_layer(used)


def graph_attention_layer(core, x_dram, y_dram, w):
    nc, ps, groups = core.nc, core.ps, core.groups
    H = 4
    CH = H * KC
    WC = H * D + H
    THIRDS = ((0, 344), (344, 344), (688, WC - 688))
    ctx = ExitStack()
    with ctx:
        sb = lambda n, shape, dt=F32: ctx.enter_context(nc.sbuf_tensor(f"l2_{n}", shape, dt))
        g_w_hi, g_w_lo = sb("g_w_hi", [P, H, KC, D], F32R), sb("g_w_lo", [P, H, KC, D], F32R)
        wh_w_hi, wh_w_lo = sb("wh_w_hi", [P, KC, WC], F32R), sb("wh_w_lo", [P, KC, WC], F32R)
        aw_hi, aw_lo = sb("aw_hi", [P, CH, D], F32R), sb("aw_lo", [P, CH, D], F32R)
        sq_hi, sq_lo = sb("sq_hi", [P, 3, KC, D], F32R), sb("sq_lo", [P, 3, KC, D], F32R)
        v_col = sb("v_col", [P, H, KC])
        wh_bias = sb("wh_bias", [P, WC])
        half_gbias = sb("half_gbias", [P, KC])

        graph_attention_weights(core, w, g_w_hi, g_w_lo, wh_w_hi, wh_w_lo, aw_hi, aw_lo, sq_hi, sq_lo, v_col,
                                wh_bias, half_gbias)

        ln = LayerNorm(core, ctx, "l2", x_dram, want_f32=True)
        adj_u8 = sb("adj_u8", [P, 2, PAIRS, S], U8)
        adj = sb("adj", [P, 2, PAIRS, S])
        gT = sb("gT", [P, H, KC, TOK])
        wh = sb("wh", [P, PAIRS, WC])
        c_diag = sb("c_diag", [P, PAIRS, H, S])
        th = sb("th", [P, PAIRS, H, S])
        a_bd = sb("a_bd", [P, PAIRS, H, 2, S])
        cat_hi, cat_lo = sb("cat_hi", [P, CH, TOK], F32R), sb("cat_lo", [P, CH, TOK], F32R)
        ha_hi, ha_lo = sb("ha_hi", [P, KC, TOK], F32R), sb("ha_lo", [P, KC, TOK], F32R)
        hf = sb("hf", [P, 2, KC, TOK])
        hf_hi, hf_lo = sb("hf_hi", [P, 2, KC, TOK], F32R), sb("hf_lo", [P, 2, KC, TOK], F32R)
        gate = sb("gate", [P, KC, TOK])
        diff = sb("diff", [P, KC, TOK])
        part = sb("part", [P, KC, TOK])
        yT = sb("yT", [P, KC, TOK])
        x_res = sb("x_res", [P, 2, PAIRS, D])
        y = sb("y", [P, 2, PAIRS, D])

        s, d = core.named_signal, core.named_dma_signal
        x_res_loaded, adj_loaded, y_stored = d("x_res_loaded"), d("adj_loaded"), d("y_stored")
        adj_ready = s("mask_ready")
        g_in_psum, g_ready = s("g_in_psum", H), s("g_ready", H)
        wh_in_psum, wh_ready = s("wh_in_psum", 6), s("wh_ready", 6)
        hf_in_psum, hf_hi_ready, hf_lo_ready = s("q_in_psum"), s("q_ready"), s("k_bd_dve_ready")
        c_diag_ready = s("c_diag_ready")
        scores_in_psum = s("scores_in_psum_of_1", 1)
        th_ready, a_pool_ready, a_dve_ready = s("prob_ready_of_1", 1), s("a_pool_ready"), s("a_dve_ready")
        hp_in_psum, cat_hi_ready, cat_lo_ready = s("hp_in_psum", H), s("cat_hi_ready", H), s("cat_lo_ready", H)
        ha_in_psum, ha_hi_ready, ha_lo_ready = s("o_in_psum"), s("oT_hi_ready"), s("oT_lo_ready")
        gate_in_psum, gate_ready = s("gate_in_psum"), s("gate_ready")
        blend_steps = s("blend_steps", 3)
        yT_in_psum, y_ready = s("proj_in_psum"), s("y_ready")
        used = ln.used + ["x_res_loaded", "adj_loaded", "y_stored", "mask_ready", "g_in_psum", "g_ready", "wh_in_psum",
                          "wh_ready", "q_in_psum", "q_ready", "k_bd_dve_ready", "c_diag_ready", "scores_in_psum_of_1",
                          "prob_ready_of_1", "a_pool_ready", "a_dve_ready", "hp_in_psum", "cat_hi_ready",
                          "cat_lo_ready", "o_in_psum", "oT_hi_ready", "oT_lo_ready", "gate_in_psum", "gate_ready",
                          "blend_steps", "proj_in_psum", "y_ready"]
        B_HT = B_YT = 0
        B_G, B_WH, B_HF = (1, 2, 3, 1), (2, 3, 1, 2, 3, 1), 2
        B_GATE, B_S = 3, 4
        B_HP, B_HA = (5, 6, 5, 6), 7
        zeroed = core.once("setup_zeroed_l2")
        halves = lambda bank: ps[:, bank, :].rearrange("p (c t) -> p c t", c=KC)

        block = ctx.enter_context(nc.Block())

        @block.sync
        def _(sp):
            def step(g):
                if g.exists(groups):
                    ln.load(sp, g)
                b1 = g.back(1)
                if b1.exists(groups):
                    after(sp, adj_ready, b1.back(2), apart=core)
                    sp.dma_start(adj_u8[:, b1.slot], w["adjT"][bass.ds(b1.times(TOK), TOK), :]
                                 .rearrange("(p q) t -> q p t", q=P)).then_inc(adj_loaded[b1.slot].sem, 16)
                r = g.back(2)
                if r.exists(groups):
                    after(sp, y_ready, r.back(2), apart=core)
                    sp.dma_start(x_res[:, r.slot], tokens_of(x_dram, r)).then_inc(x_res_loaded[r.slot].sem, 16)
                e = g.back(3)
                if e.exists(groups):
                    after(sp, y_ready, e, apart=core)
                    sp.dma_start(tokens_of(y_dram, e), y[:, e.slot]).then_inc(y_stored[e.slot].sem, 16)

            run_steps(sp, step, groups, 3)
            for e in (groups - 2, groups - 1):
                after_dma(sp, y_stored, Group(None, e))

        @block.gpsimd
        def _(pool):
            nc.gpsimd.memset(a_bd[:], 0.0).then_inc(zeroed.sem, 1)
            pool.wait_ge(zeroed.sem, 1)

            def step(g):
                c2, b1 = g.back(2), g.back(1)
                if g.exists(groups):
                    ln.root(pool, g)
                if c2.exists(groups):
                    after(pool, th_ready, c2)
                    after(pool, hp_in_psum, c2.back(1))
                    nc.gpsimd.tensor_tensor(a_bd[0:S, :, :, 0, :], th[0:S],
                                            adj[0:S, c2.slot].unsqueeze(2).to_broadcast([S, PAIRS, H, S]),
                                            ALU.mult).then_inc(a_pool_ready.sem, 1)
                if b1.exists(groups):
                    after_dma(pool, adj_loaded, b1)
                    after(pool, a_dve_ready, b1.back(2), apart=core)
                    nc.gpsimd.tensor_scalar(adj[:, b1.slot], adj_u8[:, b1.slot], 1.0, None,
                                            ALU.mult).then_inc(adj_ready.sem, 1)
                    after(pool, wh_ready, b1)
                    after(pool, scores_in_psum, b1.back(1))
                    for p in range(PAIRS):
                        last = nc.gpsimd.tensor_tensor(
                            c_diag[:, p], wh[:, p, H * D:WC].unsqueeze(2).to_broadcast([P, H, S]),
                            core.eye64[:].unsqueeze(1).to_broadcast([P, H, S]), ALU.mult)
                    last.then_inc(c_diag_ready.sem, 1)

            run_steps(pool, step, groups, 2)

        @block.scalar
        def _(act):
            def step(g):
                c2, b1 = g.back(2), g.back(1)
                if c2.exists(groups):
                    after(act, scores_in_psum, c2)
                    after(act, a_pool_ready, c2.back(1))
                    after(act, a_dve_ready, c2.back(1))
                    nc.scalar.activation(th[:], ps[:, B_S, :].rearrange("p (q h t) -> p q h t", q=PAIRS, h=H),
                                         ACT.Tanh).then_inc(th_ready.sem, 1)
                if c2.exists(groups):
                    after(act, ha_in_psum, c2.back(1))
                    for h in range(H):
                        after(act, hp_in_psum, c2, h + 1)
                        nc.scalar.activation(cat_hi[:, h * KC:(h + 1) * KC], halves(B_HP[h]),
                                             ACT.Relu).then_inc(cat_hi_ready.sem, 1)
                if g.exists(groups):
                    ln.apply(act, g)
                if c2.exists(groups):
                    after(act, ha_in_psum, c2)
                    after(act, gate_in_psum, c2.back(1))
                    nc.scalar.activation(ha_hi[:], halves(B_HA), ACT.Copy).then_inc(ha_hi_ready.sem, 1)
                if b1.exists(groups):
                    after(act, hf_in_psum, b1)
                    after(act, gate_in_psum, b1.back(2))
                    after(act, blend_steps, b1.back(2), 1)
                    nc.scalar.activation(hf_hi[:, b1.slot], halves(B_HF), ACT.Copy)
                    nc.scalar.activation(hf[:, b1.slot], halves(B_HF), ACT.Copy).then_inc(hf_hi_ready.sem, 1)
                if c2.exists(groups):
                    after(act, gate_in_psum, c2)
                    after(act, blend_steps, c2.back(1), 2)
                    for c in range(KC):
                        last = nc.scalar.activation(gate[:, c], ps[:, B_GATE, c * TOK:(c + 1) * TOK], ACT.Tanh,
                                                    bias=half_gbias[:, c:c + 1], scale=0.5)
                    last.then_inc(gate_ready.sem, 1)
                if g.exists(groups):
                    after(act, scores_in_psum, g.back(2))
                    ln.evacuate_hi(act, g, B_HT)

            run_steps(act, step, groups, 2)

        @block.vector
        def _(dve):
            dve.wait_ge(zeroed.sem, 1)

            def step(g):
                c2, b1, e = g.back(2), g.back(1), g.back(3)

                def evacuate_g(h):
                    after(dve, g_in_psum, b1, h + 1)
                    if h == 0:
                        after(dve, scores_in_psum, b1.back(1))
                    nc.vector.tensor_tensor(gT[:, h], halves(B_G[h]), v_col[:, h].unsqueeze(2).to_broadcast([P, KC, TOK]),
                                            ALU.add).then_inc(g_ready.sem, 1)

                def evacuate_wh(i):
                    p, (c0, n) = i // 3, THIRDS[i % 3]
                    after(dve, wh_in_psum, b1, i + 1)
                    if i == 0:
                        after(dve, hp_in_psum, b1.back(1))
                        after(dve, c_diag_ready, b1.back(1))
                    nc.vector.tensor_tensor(wh[:, p, c0:c0 + n], ps[:, B_WH[i], 0:n], wh_bias[:, c0:c0 + n],
                                            ALU.add).then_inc(wh_ready.sem, 1)

                def split_hp(h):
                    after(dve, cat_hi_ready, c2, h + 1)
                    if h == 0:
                        after(dve, ha_in_psum, c2.back(1))
                    nc.vector.scalar_tensor_tensor(
                        out=cat_lo[:, h * KC:(h + 1) * KC], in0=halves(B_HP[h]), scalar=0.0,
                        in1=cat_hi[:, h * KC:(h + 1) * KC], op0=ALU.max, op1=ALU.subtract).then_inc(cat_lo_ready.sem, 1)

                if e.exists(groups):
                    after(dve, gate_ready, e)
                    nc.vector.tensor_tensor(diff[:], hf[:, e.slot], halves(B_HA), ALU.subtract).then_inc(blend_steps.sem, 1)
                    after(dve, blend_steps, e, 1)
                    nc.vector.scalar_tensor_tensor(out=part[:], in0=gate[:], scalar=1.0, in1=diff[:], op0=ALU.add,
                                                   op1=ALU.mult).then_inc(blend_steps.sem, 1)
                    after(dve, blend_steps, e, 2)
                    after(dve, yT_in_psum, e.back(1))
                    nc.vector.scalar_tensor_tensor(out=yT[:], in0=part[:], scalar=0.5, in1=halves(B_HA), op0=ALU.mult,
                                                   op1=ALU.add).then_inc(blend_steps.sem, 1)
                if g.exists(groups):
                    ln.statistics(dve, g, first=True)
                if c2.exists(groups):
                    after(dve, th_ready, c2)
                    after(dve, adj_ready, c2)
                    after(dve, hp_in_psum, c2.back(1))
                    nc.vector.tensor_tensor(a_bd[S:P, :, :, 1, :], th[S:P],
                                            adj[S:P, c2.slot].unsqueeze(2).to_broadcast([S, PAIRS, H, S]),
                                            ALU.mult).then_inc(a_dve_ready.sem, 1)
                if g.exists(groups):
                    ln.statistics(dve, g, first=False)
                if b1.exists(groups):
                    evacuate_g(0)
                    evacuate_g(1)
                if e.exists(groups):
                    after(dve, yT_in_psum, e)
                    after_dma(dve, x_res_loaded, e)
                    after_dma(dve, y_stored, e.back(2))
                    nc.vector.tensor_tensor(y[:, e.slot], ps[:, B_YT, :].rearrange("q (p d) -> q p d", p=PAIRS),
                                            x_res[:, e.slot], ALU.add).then_inc(y_ready.sem, 1)
                if b1.exists(groups):
                    evacuate_g(2)
                    evacuate_g(3)
                if g.exists(groups):
                    ln.shifts(dve, g)
                if c2.exists(groups):
                    for h in range(H):
                        split_hp(h)
                if b1.exists(groups):
                    for i in range(6):
                        evacuate_wh(i)
                if c2.exists(groups):
                    after(dve, ha_hi_ready, c2)
                    after(dve, gate_in_psum, c2.back(1))
                    nc.vector.tensor_tensor(ha_lo[:], halves(B_HA), ha_hi[:], ALU.subtract).then_inc(ha_lo_ready.sem, 1)
                if b1.exists(groups):
                    after(dve, hf_hi_ready, b1)
                    after(dve, gate_in_psum, b1.back(2))
                    nc.vector.tensor_tensor(hf_lo[:, b1.slot], halves(B_HF), hf_hi[:, b1.slot],
                                            ALU.subtract).then_inc(hf_lo_ready.sem, 1)
                if g.exists(groups):
                    after(dve, scores_in_psum, g.back(2))
                    ln.evacuate_lo(dve, g, B_HT)

            run_steps(dve, step, groups, 3)

        @block.tensor
        def _(pe):
            pe.wait_ge(zeroed.sem, 1)

            def step(g):
                c2, b1, e = g.back(2), g.back(1), g.back(3)

                def product_T(bank, terms):
                    for oc in range(KC):
                        k = 0
                        chunks = [(wt, src, c) for wt, src, n in terms for c in range(n)]
                        for wt, src, c in chunks:
                            last = mm3(nc, ps[:, bank, oc * TOK:(oc + 1) * TOK], wt, src, k == 0, k == len(chunks) - 1,
                                       lambda a: a[:, c, oc * P:(oc + 1) * P], lambda a: a[:, c, :])
                            k += 1
                    return last

                if b1.exists(groups):
                    hT = (ln.hT_hi[:, b1.slot], ln.hT_lo[:, b1.slot])

                def product_g(h):
                    if h == 0:
                        after(pe, wh_ready, b1.back(1))
                    elif h == 1:
                        after(pe, hf_lo_ready, b1.back(1))
                    elif h == 2:
                        after(pe, wh_ready, b1.back(1), 5)
                        after(pe, gate_ready, b1.back(2))
                    else:
                        after(pe, g_ready, b1, 1)
                    product_T(B_G[h], [((g_w_hi[:, h], g_w_lo[:, h]), hT, KC)]).then_inc(g_in_psum.sem, 1)

                def product_hp(h):
                    if h < 2:
                        after(pe, cat_lo_ready, c2.back(1), h + 3)
                    else:
                        after(pe, cat_lo_ready, c2, h - 1)
                    for c in range(KC):
                        for p in range(PAIRS):
                            col = c * TOK + p * P
                            last = nc.tensor.matmul(ps[:, B_HP[h], col:col + P],
                                                    wh[:, p, h * D + c * P:h * D + (c + 1) * P],
                                                    a_bd[:, p, h].rearrange("q b t -> q (b t)"), start=True, stop=True)
                    last.then_inc(hp_in_psum.sem, 1)

                if c2.exists(groups):
                    u = c2.slot
                    after(pe, g_ready, c2)
                    after(pe, c_diag_ready, c2)
                    after(pe, th_ready, c2.back(1))
                    for p in range(PAIRS):
                        cols = slice(p * H * S, (p + 1) * H * S)
                        nc.tensor.matmul(ps[:, B_S, cols], core.same_batch[:],
                                         c_diag[:, p].rearrange("q h t -> q (h t)"), start=True, stop=False,
                                         skip_group_check=True)
                        for b in range(2):
                            t0 = p * P + b * S
                            for c in range(KC):
                                last = nc.tensor.matmul(ps[b * S:(b + 1) * S, B_S, cols], ln.hT[:, u, c, t0:t0 + S],
                                                        gT[:, :, c, t0:t0 + S], start=False, stop=True,
                                                        skip_group_check=True)
                    last.then_inc(scores_in_psum.sem, 1)
                if b1.exists(groups):
                    after(pe, ln.hT_hi_ready, b1)
                    after(pe, ln.hT_lo_ready, b1)
                    product_g(0)
                    product_g(1)
                if e.exists(groups):
                    after(pe, blend_steps, e)
                    after(pe, ln.hT_lo_ready, e.back(-2))
                    for p in range(PAIRS):
                        for c in range(KC):
                            last = nc.tensor.transpose(ps[:, B_YT, p * D + c * P:p * D + (c + 1) * P],
                                                       yT[:, c, p * P:(p + 1) * P], core.ident)
                    last.then_inc(yT_in_psum.sem, 1)
                if b1.exists(groups):
                    product_g(2)
                    product_g(3)
                if c2.exists(groups):
                    after(pe, a_pool_ready, c2)
                    after(pe, a_dve_ready, c2)
                    after(pe, wh_ready, c2)
                    for h in range(H):
                        product_hp(h)
                if b1.exists(groups):
                    for i in range(6):
                        p, (c0, n) = i // 3, THIRDS[i % 3]
                        if i < 3:
                            after(pe, g_ready, b1, i + 2)
                        else:
                            after(pe, wh_ready, b1, i - 2)
                        for c in range(KC):
                            last = mm3(nc, ps[:, B_WH[i], 0:n], hT, (wh_w_hi, wh_w_lo), c == 0, c == KC - 1,
                                       lambda a: a[:, c, p * P:(p + 1) * P], lambda a: a[:, c, c0:c0 + n])
                        last.then_inc(wh_in_psum.sem, 1)
                if c2.exists(groups):
                    after(pe, cat_lo_ready, c2)
                    after(pe, blend_steps, c2.back(1))
                    product_T(B_HA, [((aw_hi, aw_lo), (cat_hi, cat_lo), CH)]).then_inc(ha_in_psum.sem, 1)
                if b1.exists(groups):
                    after(pe, wh_ready, b1, 4)
                    product_T(B_HF, [((sq_hi[:, 0], sq_lo[:, 0]), hT, KC)]).then_inc(hf_in_psum.sem, 1)
                if c2.exists(groups):
                    after(pe, wh_ready, b1 if b1.exists(groups) else c2, 5)
                    after(pe, hf_lo_ready, c2)
                    after(pe, ha_lo_ready, c2)
                    product_T(B_GATE, [((sq_hi[:, 1], sq_lo[:, 1]), (hf_hi[:, c2.slot], hf_lo[:, c2.slot]), KC),
                                       ((sq_hi[:, 2], sq_lo[:, 2]), (ha_hi, ha_lo), KC)]).then_inc(gate_in_psum.sem, 1)
                if g.exists(groups):
                    after(pe, y_ready, g.back(3))
                    ln.transpose(pe, g, B_HT)

            run_steps(pe, step, groups, 3)
    core.end_layer(used)


def graph_attention_weights(core, w, g_w_hi, g_w_lo, wh_w_hi, wh_w_lo, aw_hi, aw_lo, sq_hi, sq_lo, v_col, wh_bias,
                            half_gbias):
    nc, ps = core.nc, core.ps
    H = 4
    CH = H * KC
    HD = H * D
    with ExitStack() as ctx:
        sb = lambda n, shape, dt=F32: ctx.enter_context(nc.sbuf_tensor(f"l2_stage_{n}", shape, dt))
        w_nat = sb("w_nat", [P, CH, D])
        attn = sb("attn", [P, CH, D])
        attnT = sb("attnT", [P, CH, D])
        wh_w = sb("wh_w", [P, KC, HD + H])
        aw = sb("aw", [P, CH, D])
        sq = sb("sq", [P, 3, KC, D])
        b_col = sb("b_col", [P, CH])
        gbias = sb("gbias", [P, KC])
        attn_w = sb("attn_w", [P, CH, D])
        vec = sb("vec", [P, 2, CH])
        loaded = core.once("setup_loaded_l2")
        staged = core.once("setup_staged_l2")
        y_in_psum, y_out = core.once("setup_attn_w_psum_l2"), core.once("setup_attn_w_l2")
        g_in_psum = core.once("setup_g_psum_l2")
        wr_ready = core.once("setup_wr_l2")
        hi, lo = core.once("setup_hi_l2"), core.once("setup_lo_l2")
        halves = lambda bank: ps[:, bank, :].rearrange("p (c n) -> p c n", c=KC)
        B_VEC, B_VEC2 = 4, 5

        block = ctx.enter_context(nc.Block())

        @block.sync
        def _(sp):
            for t, name in ((w_nat, "W"), (attnT, "attnT"), (attn, "attn")):
                sp.dma_start(t[:], rows(w[name])).then_inc(loaded.sem, 16)
            sp.dma_start(b_col[:], w["b_col"]).then_inc(loaded.sem, 16)
            sp.dma_start(wh_w[:, :, 0:HD], rows(w["WT"])).then_inc(staged.sem, 16)
            sp.dma_start(aw[:], rows(w["AwT"])).then_inc(staged.sem, 16)
            for i, name in enumerate(("fcT", "g1T", "g2T")):
                sp.dma_start(sq[:, i], rows(w[name])).then_inc(staged.sem, 16)
            sp.dma_start(wh_bias[:, 0:HD], everywhere(w["b"])).then_inc(staged.sem, 16)
            sp.dma_start(gbias[:], w["gbias"]).then_inc(staged.sem, 16)

        @block.tensor
        def _(pe):
            pe.wait_ge(loaded.sem, 64)
            for h in range(H):
                for oc in range(KC):
                    for pc in range(KC):
                        k = h * KC + pc
                        nc.tensor.matmul(ps[:, h, oc * D:(oc + 1) * D], attnT[:, k, oc * P:(oc + 1) * P], w_nat[:, k, :],
                                         start=pc == 0, stop=pc == KC - 1)
            for i, m in ((0, attn), (1, attnT)):
                for h in range(H):
                    for rc in range(KC):
                        for c in range(KC):
                            k = h * KC + c
                            col = i * CH + h * KC + rc
                            last = nc.tensor.matmul(ps[:, B_VEC, col:col + 1], m[:, k, rc * P:(rc + 1) * P],
                                                    b_col[:, k:k + 1], start=c == 0, stop=c == KC - 1)
            last.then_inc(y_in_psum.sem, 1)
            pe.wait_ge(y_out.sem, H + 1)
            for h in range(H):
                for jc in range(KC):
                    for c in range(KC):
                        k = h * KC + c
                        nc.tensor.matmul(ps[:, h, jc * D:(jc + 1) * D], w_nat[:, k, jc * P:(jc + 1) * P], attn_w[:, k, :],
                                         start=c == 0, stop=c == KC - 1)
            for i in range(2):
                for h in range(H):
                    for jc in range(KC):
                        for c in range(KC):
                            k = h * KC + c
                            col = i * CH + h * KC + jc
                            nc.tensor.matmul(ps[:, B_VEC2, col:col + 1], w_nat[:, k, jc * P:(jc + 1) * P],
                                             vec[:, i, k:k + 1], start=c == 0, stop=c == KC - 1)
            for h in range(H):
                for c in range(KC):
                    k = h * KC + c
                    last = nc.tensor.matmul(ps[:, B_VEC2, 2 * CH + h:2 * CH + h + 1],
                                            b_col[:, k:k + 1].to_broadcast([P, P]), vec[:, 1, k:k + 1],
                                            start=c == 0, stop=c == KC - 1)
            last.then_inc(g_in_psum.sem, 1)

        @block.scalar
        def _(act):
            act.wait_ge(y_in_psum.sem, 1)
            for h in range(H):
                nc.scalar.activation(attn_w[:, h * KC:(h + 1) * KC], halves(h), ACT.Copy).then_inc(y_out.sem, 1)
            act.wait_ge(staged.sem, 112)
            nc.scalar.activation(sq_hi[:], sq[:], ACT.Copy).then_inc(hi.sem, 1)
            nc.scalar.activation(aw_hi[:], aw[:], ACT.Copy).then_inc(hi.sem, 1)
            act.wait_ge(g_in_psum.sem, 1)
            for h in range(H):
                nc.scalar.activation(g_w_hi[:, h], halves(h), ACT.Copy).then_inc(hi.sem, 1)
            act.wait_ge(wr_ready.sem, 1)
            nc.scalar.activation(wh_w_hi[:], wh_w[:], ACT.Copy).then_inc(hi.sem, 1)
            nc.scalar.activation(half_gbias[:], gbias[:], ACT.Copy, scale=0.5)

        @block.vector
        def _(dve):
            dve.wait_ge(y_in_psum.sem, 1)
            nc.vector.tensor_copy(vec[:], ps[:, B_VEC, 0:2 * CH].rearrange("p (i k) -> p i k", i=2)).then_inc(y_out.sem, 1)
            dve.wait_ge(hi.sem, 1)
            nc.vector.tensor_tensor(sq_lo[:], sq[:], sq_hi[:], ALU.subtract)
            dve.wait_ge(hi.sem, 2)
            nc.vector.tensor_tensor(aw_lo[:], aw[:], aw_hi[:], ALU.subtract)
            dve.wait_ge(g_in_psum.sem, 1)
            nc.vector.tensor_copy(v_col[:], ps[:, B_VEC2, 0:CH].rearrange("p (h c) -> p h c", h=H))
            nc.vector.tensor_copy(wh_bias[:, HD:HD + H], ps[:, B_VEC2, 2 * CH:2 * CH + H])
            nc.vector.tensor_copy(wh_w[:, :, HD:HD + H],
                                  ps[:, B_VEC2, CH:2 * CH].rearrange("p (h c) -> p c h", h=H)).then_inc(wr_ready.sem, 1)
            for h in range(H):
                dve.wait_ge(hi.sem, 3 + h)
                nc.vector.tensor_tensor(g_w_lo[:, h], halves(h), g_w_hi[:, h], ALU.subtract)
            dve.wait_ge(hi.sem, 3 + H)
            nc.vector.tensor_tensor(wh_w_lo[:], wh_w[:], wh_w_hi[:], ALU.subtract)


def build(nc, a, out):
    hidden = [nc.dram_tensor(f"hidden_{i}", (GROUPS * TOK, D), F32, kind="Internal").ap() for i in range(3)]
    x = [a["x"]] + hidden + [out]
    with ExitStack() as ctx:
        core = Core(nc, ctx, GROUPS)
        load_constants(core, ctx, a["constants"])
        attention_layer(core, "l0", x[0], x[1], a["adj"],
                        (a["L0_WqT"], a["L0_WkT"], a["L0_WvT"], a["L0_WoT"]),
                        (a["L0_bq"], a["L0_bk"], a["L0_bv"], a["L0_bo"]), 8, core.static_mask)
        attention_layer(core, "l1", x[1], x[2], a["adj"],
                        (a["L1_Wq"], a["L1_Wk"], a["L1_Wv"], a["L1_Wo"]),
                        (None, None, None, a["L1_bo"]), 4, None)
        graph_attention_layer(core, x[2], x[3],
                              {"adjT": a["adjT"], **{k[3:]: v for k, v in a.items() if k.startswith("L2_")}})
        gated_graph_layer(core, x[3], x[4], a["adj"],
                          {k: a["L3_w_" + k] for k in ("map", "qT", "kT", "mapT", "gmap", "gcn_WT")},
                          {k: a["L3_b_" + k] for k in ("map", "q", "k", "gmap", "map_row")})


def layout(t):
    n = {k: np.ascontiguousarray(v) for k, v in t.items()}
    T = lambda w: np.ascontiguousarray(w.T)
    col = lambda b: np.ascontiguousarray(b.reshape(-1, P).T)
    arrays = {
        "x": n["x"].reshape(-1, D),
        "adj": n["adj"].reshape(-1, S),
        "L0_WqT": T(n["L0_gnn_Wq"]), "L0_WkT": T(n["L0_gnn_Wk"]), "L0_WvT": T(n["L0_gnn_Wv"]), "L0_WoT": T(n["L0_gnn_Wo"]),
        "L0_bq": col(n["L0_gnn_bq"]), "L0_bk": col(n["L0_gnn_bk"]), "L0_bv": col(n["L0_gnn_bv"]), "L0_bo": n["L0_gnn_bo"],
        "L1_Wq": n["L1_gnn_Wq"], "L1_Wk": n["L1_gnn_Wk"], "L1_Wv": n["L1_gnn_Wv"], "L1_Wo": n["L1_gnn_Wo"],
        "L1_bo": n["L1_gnn_bo"],
        "L2_W": n["L2_gnn_W"].reshape(-1, D), "L2_WT": T(n["L2_gnn_W"].reshape(-1, D)),
        "L2_attn": n["L2_gnn_attn"].reshape(-1, D),
        "L2_attnT": np.ascontiguousarray(n["L2_gnn_attn"].transpose(0, 2, 1)).reshape(-1, D),
        "L2_AwT": T(n["L2_gnn_A_w"]), "L2_fcT": T(n["L2_gnn_fc_w"]), "L2_g1T": T(n["L2_gnn_g1_w"]),
        "L2_g2T": T(n["L2_gnn_g2_w"]), "L2_b": n["L2_gnn_bW"].reshape(-1), "L2_b_col": col(n["L2_gnn_bW"]),
        "L2_gbias": col(n["L2_gnn_gbias"]),
        "adjT": np.ascontiguousarray(n["adj"].transpose(0, 2, 1)).reshape(-1, S),
        "L3_w_map": n["L3_gnn_map_w"], "L3_w_mapT": T(n["L3_gnn_map_w"]), "L3_w_qT": T(n["L3_gnn_q_w"]),
        "L3_w_kT": T(n["L3_gnn_k_w"]), "L3_w_gmap": n["L3_gnn_gcn_map_w"], "L3_w_gcn_WT": T(n["L3_gnn_gcn_W"]),
        "L3_b_map": col(n["L3_gnn_map_b"]), "L3_b_q": col(n["L3_gnn_q_b"]), "L3_b_k": col(n["L3_gnn_k_b"]),
        "L3_b_gmap": col(n["L3_gnn_gcn_map_b"]), "L3_b_map_row": n["L3_gnn_map_b"],
        "constants": constants(),
    }
    return arrays


def kernel(**inputs):
    import concourse.bacc as bacc
    from concourse.bass_utils import run_bass_kernel_spmd

    nc = bacc.Bacc("TRN2", target_bir_lowering=False, num_devices=1)
    arrays = layout(inputs)
    a = {k: nc.dram_tensor(k, v.shape, mybir.dt.from_np(v.dtype), kind="ExternalInput").ap()
         for k, v in arrays.items()}
    out = nc.dram_tensor("out", (GROUPS * TOK, D), F32, kind="ExternalOutput").ap()
    build(nc, a, out)
    r = run_bass_kernel_spmd(nc, [arrays], core_ids=[0])
    return r.results[0]["out"].reshape(inputs["x"].shape)
```
